# Optimizing a Trainium2 kernel written in Bass

```python
import numpy as np
import jax
import jax.numpy as jnp

def _softmax(x, axis=-1):
    return jax.nn.softmax(x, axis=axis)

def _gelu(x):
    return jax.nn.gelu(x, approximate=True)

def _silu(x):
    return jax.nn.silu(x)

def _sigmoid(x):
    return jax.nn.sigmoid(x)

def _layernorm(x, axis=-1, eps=1e-05):
    m = jnp.mean(x, axis=axis, keepdims=True)
    v = jnp.var(x, axis=axis, keepdims=True)
    return (x - m) / jnp.sqrt(v + eps)

def _scatter_add(tgt, idx, src, axis=0):
    return tgt.at[idx].add(src)

def _segment_sum(src, seg, n):
    return jax.ops.segment_sum(src, seg, n)
kernel_name = 'mk_flamingo_gated_d2_seqx_r8_6e9c35'

def setup_inputs(seed: int=0):
    np.random.seed(seed)
    _w = jnp.asarray

    def _rec_inputs():
        import jax
        import jax.numpy as jnp
        _rk = jax.random.key(seed)
        x = 0.0001212 + 1 * jax.random.normal(jax.random.fold_in(_rk, 1), (8, 128, 512), jnp.float32)
        _lenS = 128 - jax.random.randint(jax.random.fold_in(_rk, 7), (8,), 0, max(1, 128 // 4) + 1, jnp.int32)
        _lenS2 = 128 - jax.random.randint(jax.random.fold_in(_rk, 8), (8,), 0, max(1, 128 // 4) + 1, jnp.int32)
        _ctx_4096P = jax.random.normal(jax.random.fold_in(_rk, 11), (8, 16, 512), jnp.float32)
        _ctx_4096c = jax.random.dirichlet(jax.random.fold_in(_rk, 511), 0.3 * jnp.ones((16,), jnp.float32), (8, 128))
        _ctx_4096t = jnp.einsum('bsk,bkd->bsd', _ctx_4096c, _ctx_4096P)
        _ctx_4096t = _ctx_4096t * jax.lax.rsqrt(jnp.mean(jnp.square(_ctx_4096t)) + 1e-12) * 0.953939
        ctx_4096 = -0.000125008 + 0.999885 * (_ctx_4096t + 0.3 * jax.random.normal(jax.random.fold_in(_rk, 611), (8, 128, 512), jnp.float32))
        _validS = jnp.arange(128)[None, :] < _lenS[:, None]
        _validS2 = jnp.arange(128)[None, :] < _lenS2[:, None]
        _causal = jnp.tril(jnp.ones((128, 128), dtype=bool))
        mask_BxSxS2_bk0 = jnp.logical_not(jnp.broadcast_to(_validS2[:, None, :], (8, 128, 128)))
        _g = jax.random.normal(jax.random.fold_in(_rk, 9001), (2, 2), jnp.float32)
        _g = jnp.sign(_g) * jnp.maximum(jnp.abs(_g), 1.0) + (_g == 0) * 1.0
        g_xattn = _g[0]
        g_ffn = _g[1]
        return (x, ctx_4096, mask_BxSxS2_bk0, g_xattn, g_ffn)
    x, ctx_4096, mask_BxSxS2_bk0, g_xattn, g_ffn = _rec_inputs()

    def _L0_xattn_setup():
        import jax, jax.numpy as jnp
        import numpy as np
        N, C, S = (16, 64, 512)
        rng = jax.random.key(seed)
        k1, k2, k3 = jax.random.split(rng, 3)
        return {'key': jax.random.normal(k1, (N, C, S), dtype=jnp.float32), 'value': jax.random.normal(k2, (N, C, S), dtype=jnp.float32), 'query': jax.random.normal(k3, (N, C, S), dtype=jnp.float32)}
    _L0_xattn_all = _L0_xattn_setup()
    _L0_xattn_in = {k: v for k, v in _L0_xattn_all.items() if k in ()}
    del _L0_xattn_all

    def _L0_ffn_setup():
        import jax, jax.numpy as jnp
        import numpy as np
        IN_F = 512
        OUT_F = 512
        RANK = 8
        NUM_EXPERTS = 64
        TOP_K = 16
        ROUTER_DIM = 16
        ALPHA = 32
        SCALING = ALPHA / TOP_K
        BOTTLENECK = NUM_EXPERTS * RANK
        key = jax.random.key(seed)
        ks = jax.random.split(key, 5)
        x = jax.random.normal(ks[0], (4, 512, IN_F), dtype=jnp.float32)
        bound_a = float(np.sqrt(6.0 / IN_F))
        A_w = jax.random.uniform(ks[1], (BOTTLENECK, IN_F), jnp.float32, -bound_a, bound_a)
        B_w = jax.random.normal(ks[2], (OUT_F, BOTTLENECK), dtype=jnp.float32) * 0.02
        Wq_w = jax.random.normal(ks[3], (ROUTER_DIM, IN_F), dtype=jnp.float32) * 0.02
        keys = jax.random.normal(ks[4], (NUM_EXPERTS, ROUTER_DIM), dtype=jnp.float32) * 0.01
        return {'x': x, 'A_w': A_w, 'B_w': B_w, 'Wq_w': Wq_w, 'keys': keys}
    _L0_ffn_all = _L0_ffn_setup()
    _L0_ffn_in = {k: v for k, v in _L0_ffn_all.items() if k in ('A_w', 'B_w', 'Wq_w', 'keys')}
    del _L0_ffn_all

    def _L1_xattn_setup():
        import jax, jax.numpy as jnp
        import numpy as np
        B, LQ, LK, D, H, DH = (2, 128, 128, 512, 32, 128)
        EPS = 1e-05

        def _rmsnorm(x, weight):
            var = jnp.mean(jnp.square(x), axis=-1, keepdims=True)
            return x * jax.lax.rsqrt(var + EPS) * weight
        key = jax.random.key(seed)
        ks = jax.random.split(key, 8)
        scale = 0.02
        return {'hidden_states': jax.random.normal(ks[0], (B, LQ, D), jnp.float32), 'key_value_states': jax.random.normal(ks[1], (B, LK, D), jnp.float32), 'attention_mask': jax.random.randint(ks[2], (B, LQ, LK), 0, 2) > 0, 'position_bias': jax.random.normal(ks[3], (H, LQ, LK), jnp.float32), 'ln_weight': jnp.ones((D,), jnp.float32), 'w_q': jax.random.normal(ks[4], (H * DH, D), jnp.float32) * scale, 'w_k': jax.random.normal(ks[5], (H * DH, D), jnp.float32) * scale, 'w_v': jax.random.normal(ks[6], (H * DH, D), jnp.float32) * scale, 'w_out': jax.random.normal(ks[7], (D, H * DH), jnp.float32) * scale}
    _L1_xattn_all = _L1_xattn_setup()
    _L1_xattn_in = {k: v for k, v in _L1_xattn_all.items() if k in ('position_bias', 'ln_weight', 'w_q', 'w_k', 'w_v', 'w_out')}
    del _L1_xattn_all

    def _L1_ffn_setup():
        import jax, jax.numpy as jnp
        import numpy as np
        GROUP = 64

        def dequant_q40(w, s, out_features, in_features):
            msb = w >> 4
            lsb = (w & 15 ^ 8) - 8
            g = jnp.concatenate([msb, lsb], axis=1).reshape(-1, GROUP)
            deq = g.astype(s.dtype) * s[:, None]
            return deq.reshape(out_features, in_features)
        key = jax.random.key(seed)
        ks = jax.random.split(key, 7)
        dim, hidden = (512, 1376)
        B, S = (2, 256)

        def packed(k, din, dout):
            return jax.random.randint(k, (din * dout // GROUP // 2, GROUP), -128, 128, dtype=jnp.int32)

        def scales(k, din, dout):
            return (jax.random.uniform(k, (din * dout // GROUP,), dtype=jnp.float32) + 0.5) * 0.01
        x = jax.random.normal(ks[0], (B, S, dim), dtype=jnp.float32)
        w1 = packed(ks[1], dim, hidden)
        s1 = scales(ks[2], dim, hidden)
        w2 = packed(ks[3], hidden, dim)
        s2 = scales(ks[4], hidden, dim)
        w3 = packed(ks[5], dim, hidden)
        s3 = scales(ks[6], dim, hidden)
        return {'x': x, 'w1': w1, 's1': s1, 'w2': w2, 's2': s2, 'w3': w3, 's3': s3}
    _L1_ffn_all = _L1_ffn_setup()
    _L1_ffn_in = {k: v for k, v in _L1_ffn_all.items() if k in ('w1', 's1', 'w2', 's2', 'w3', 's3')}
    del _L1_ffn_all
    return {'x': x, 'ctx_4096': ctx_4096, 'mask_BxSxS2_bk0': mask_BxSxS2_bk0, 'g_xattn': g_xattn, 'g_ffn': g_ffn, 'L0_ffn_A_w': _L0_ffn_in['A_w'], 'L0_ffn_B_w': _L0_ffn_in['B_w'], 'L0_ffn_Wq_w': _L0_ffn_in['Wq_w'], 'L0_ffn_keys': _L0_ffn_in['keys'], 'L1_xattn_position_bias': _L1_xattn_in['position_bias'], 'L1_xattn_ln_weight': _L1_xattn_in['ln_weight'], 'L1_xattn_w_q': _L1_xattn_in['w_q'], 'L1_xattn_w_k': _L1_xattn_in['w_k'], 'L1_xattn_w_v': _L1_xattn_in['w_v'], 'L1_xattn_w_out': _L1_xattn_in['w_out'], 'L1_ffn_w1': _L1_ffn_in['w1'], 'L1_ffn_s1': _L1_ffn_in['s1'], 'L1_ffn_w2': _L1_ffn_in['w2'], 'L1_ffn_s2': _L1_ffn_in['s2'], 'L1_ffn_w3': _L1_ffn_in['w3'], 'L1_ffn_s3': _L1_ffn_in['s3']}

def reference(x, ctx_4096, mask_BxSxS2_bk0, g_xattn, g_ffn, L0_ffn_A_w, L0_ffn_B_w, L0_ffn_Wq_w, L0_ffn_keys, L1_xattn_position_bias, L1_xattn_ln_weight, L1_xattn_w_q, L1_xattn_w_k, L1_xattn_w_v, L1_xattn_w_out, L1_ffn_w1, L1_ffn_s1, L1_ffn_w2, L1_ffn_s2, L1_ffn_w3, L1_ffn_s3):
    import jax
    import jax.numpy as jnp

    def _L0_xattn_ref(key, value, query):
        import jax, jax.numpy as jnp
        import numpy as np
        N, C, S = (16, 64, 512)
        KC = key.shape[1]
        sim = jnp.einsum('ncs,nds->ncd', key, query) * KC ** (-0.5)
        sim = jax.nn.softmax(sim, axis=1)
        context = jnp.einsum('ncd,nds->ncs', sim, value)
        return context

    def _L0_ffn_ref(x, A_w, B_w, Wq_w, keys):
        import jax, jax.numpy as jnp
        import numpy as np
        IN_F = 512
        OUT_F = 512
        RANK = 8
        NUM_EXPERTS = 64
        TOP_K = 16
        ROUTER_DIM = 16
        ALPHA = 32
        SCALING = ALPHA / TOP_K
        BOTTLENECK = NUM_EXPERTS * RANK
        q = jnp.einsum('bsd,rd->bsr', x, Wq_w)
        scores = jnp.einsum('bsr,er->bse', q, keys)
        top_vals, top_idx = jax.lax.top_k(scores, TOP_K)
        top_w = jax.nn.softmax(top_vals, axis=-1)
        gate = jnp.sum(jax.nn.one_hot(top_idx, NUM_EXPERTS, dtype=top_w.dtype) * top_w[..., None], axis=-2)
        z = jnp.einsum('bsd,nd->bsn', x, A_w)
        z = z.reshape(*z.shape[:-1], NUM_EXPERTS, RANK)
        z_gated = (z * gate[..., None]).reshape(*z.shape[:-2], BOTTLENECK)
        out = jnp.einsum('bsn,on->bso', z_gated, B_w) * SCALING
        return out

    def _L1_xattn_ref(hidden_states, key_value_states, attention_mask, position_bias, ln_weight, w_q, w_k, w_v, w_out):
        import jax, jax.numpy as jnp
        import numpy as np
        B, LQ, LK, D, H, DH = (2, 128, 128, 512, 32, 128)
        EPS = 1e-05

        def _rmsnorm(x, weight):
            var = jnp.mean(jnp.square(x), axis=-1, keepdims=True)
            return x * jax.lax.rsqrt(var + EPS) * weight
        x = _rmsnorm(hidden_states, ln_weight)
        b, lq, _ = x.shape
        lk = key_value_states.shape[1]
        h_q = (x @ w_q.T).reshape(b, lq, H, DH)
        h_k = (key_value_states @ w_k.T).reshape(b, lk, H, DH)
        h_v = (key_value_states @ w_v.T).reshape(b, lk, H, DH)
        score = jnp.einsum('bqhd,bkhd->bhqk', h_q, h_k)
        score = score + position_bias[None]
        m = attention_mask[:, None]
        score = jnp.where(m, score, -jnp.inf)
        score = jax.nn.softmax(score, axis=-1)
        score = jnp.where(m, score, 0.0)
        attn = jnp.einsum('bhqk,bkhd->bqhd', score, h_v).reshape(b, lq, H * DH)
        out = attn @ w_out.T
        return hidden_states + out

    def _L1_ffn_ref(x, w1, s1, w2, s2, w3, s3):
        import jax, jax.numpy as jnp
        import numpy as np
        GROUP = 64

        def dequant_q40(w, s, out_features, in_features):
            msb = w >> 4
            lsb = (w & 15 ^ 8) - 8
            g = jnp.concatenate([msb, lsb], axis=1).reshape(-1, GROUP)
            deq = g.astype(s.dtype) * s[:, None]
            return deq.reshape(out_features, in_features)
        dim = x.shape[-1]
        hidden = w1.shape[0] * w1.shape[1] * 2 // dim
        W1 = dequant_q40(w1, s1, hidden, dim)
        W3 = dequant_q40(w3, s3, hidden, dim)
        W2 = dequant_q40(w2, s2, dim, hidden)
        a = jnp.einsum('bsd,hd->bsh', x, W1)
        b = jnp.einsum('bsd,hd->bsh', x, W3)
        h = jax.nn.silu(a) * b
        return jnp.einsum('bsh,dh->bsd', h, W2)
    x = x + jnp.tanh(g_xattn[0]) * _L0_xattn_ref(ctx_4096, ctx_4096, _layernorm(x, axis=-1))
    x = x + jnp.tanh(g_ffn[0]) * _L0_ffn_ref(_layernorm(x, axis=-1), L0_ffn_A_w, L0_ffn_B_w, L0_ffn_Wq_w, L0_ffn_keys)
    x = x + jnp.tanh(g_xattn[1]) * _L1_xattn_ref(_layernorm(x, axis=-1), ctx_4096, mask_BxSxS2_bk0, L1_xattn_position_bias, L1_xattn_ln_weight, L1_xattn_w_q, L1_xattn_w_k, L1_xattn_w_v, L1_xattn_w_out)
    x = x + jnp.tanh(g_ffn[1]) * _L1_ffn_ref(_layernorm(x, axis=-1), L1_ffn_w1, L1_ffn_s1, L1_ffn_w2, L1_ffn_s2, L1_ffn_w3, L1_ffn_s3)
    return x

_drawn_inputs = setup_inputs


def setup_inputs(seed=0):
    import zlib

    import numpy as np

    out = dict(_drawn_inputs(seed))
    spreads = {'g_ffn': (-1.0, 0.2), 'L1_xattn_ln_weight': (1.0, 0.2)}
    factors = {}
    for name, (base, spread) in spreads.items():
        noise = np.random.default_rng([zlib.crc32(name.encode()), seed]).standard_normal(out[name].shape)
        drawn = base * np.exp(spread * noise) if base else spread * noise
        out[name] = jnp.asarray(drawn.astype(out[name].dtype))
    for name, factor in factors.items():
        out[name] = (out[name] * factor).astype(out[name].dtype)
    return out
```

```python
from contextlib import ExitStack

import concourse.bass as bass
import concourse.mybir as mybir

F32 = mybir.dt.float32
F32R = mybir.dt.float32r
I32 = mybir.dt.int32
U8 = mybir.dt.uint8
ALU = mybir.AluOpType
ACT = mybir.ActivationFunctionType
AX = mybir.AxisListType

P = 128
B = 8
D = 512
DC = D // P
T = B * P
HALF = T // 2
HB = B // 2
NE, RANK, TOPK, RD = 64, 8, 16, 16
LORA_SCALE = 32 / TOPK
HEADS, DH = 32, 128
PAIRS = HEADS // 2
HID = 1376
HC = (HID + P - 1) // P
CHUNK = 2 * DC * P + D
SHIFTS = 10
EPS = 1e-5
FAR = 1e30
LOWEST = -3.0e38
TAKEN = -1.0e38

QK0, QK1, WV, WO = range(4)
BLK = 1024
(LN1_T, SIM, CONTEXT, LN2_T, ROUTE, EXPERTS, GATED_T, MIX, LN3_T) = range(9)


def gated_layers(nc, x, ctx, ctxT, mask, small, wq_r, keysT, ab, weights, bias, words, scales, out):
    with ExitStack() as stack:
        def sb(name, shape, dt=F32):
            return stack.enter_context(nc.sbuf_tensor(name, shape, dt))

        def sem(name):
            return stack.enter_context(nc.semaphore(name))

        PS = [stack.enter_context(nc.psum_tensor(f"ps{i}", [P, 512], F32)) for i in range(8)]

        X = sb("X", [P, B, D])
        XN = sb("XN", [P, B, D])
        xT_hi = sb("xT_hi", [P, DC, T], F32R)
        xT_lo = sb("xT_lo", [P, DC, T], F32R)
        cT_hi = sb("cT_hi", [P, DC, T], F32R)
        cT_lo = sb("cT_lo", [P, DC, T], F32R)
        RAW1 = sb("RAW1", [P, 4096])
        RAW2 = sb("RAW2", [P, 4096])
        R = sb("R", [P, 19456], F32R)

        ident = sb("ident", [P, P])
        par = sb("par", [P, 8])
        gate = sb("gate", [P, 4])
        wqr, kyT = XN[0:RD, 6, :], XN[0:RD, 7, 0:NE]
        stat = sb("stat", [P, B, 6])
        mv = sb("mv", [P, B, 2])
        vareps = sb("vareps", [P, B])
        mhalf = sb("mhalf", [P, B])
        rstd = sb("rstd", [P, B])
        nmr = sb("nmr", [P, B])
        rms = sb("rms", [P, B])
        negmax = sb("negmax", [P, B])
        esum = sb("esum", [P, B])
        rsum = sb("rsum", [P, B])
        top = sb("top", [P, B, 16])
        keep = sb("keep", [P, B])
        u_max = sb("u_max", [P, HB])
        u_nmx = sb("u_nmx", [P, HB])
        u_sum = sb("u_sum", [P, HB])
        u_rs = sb("u_rs", [P, HB])

        def cut(t, at, *dims):
            n = 1
            for d in dims:
                n *= d
            v = t[:, at:at + n]
            if len(dims) == 2:
                v = v.rearrange("p (a b) -> p a b", a=dims[0])
            if len(dims) == 3:
                v = v.rearrange("p (a b c) -> p a b c", a=dims[0], b=dims[1])
            return v

        c_hi, c_lo = cut(R, 0, B, D), cut(R, 4096, B, D)
        zT_hi, zT_lo = cut(R, 0, DC, T), cut(R, 4096, DC, T)
        a_hi, a_lo = cut(R, 8192, DC, D), cut(R, 10240, DC, D)
        b_hi, b_lo = cut(R, 12288, DC, D), cut(R, 14336, DC, D)
        p_hi, p_lo = cut(R, 16384, B, P), cut(R, 17408, B, P)
        g_hi, g_lo = cut(R, 18432, DC, NE), cut(R, 18688, DC, NE)
        def ab_part(half):
            def part(c):
                at = (8192, 12288)[c // 2] + 2048 * half + 1024 * (c % 2)
                return R[:, at:at + 1024]
            return part

        v_hi, v_lo = cut(R, 0, B, 256), cut(R, 2048, B, 256)
        at_hi, at_lo = cut(R, 4096, 2, T), cut(R, 6144, 2, T)
        w_hi = [R[:, 8192:9216], R[:, 12288:13312], R[:, 10240:11264], R[:, 14336:15360]]
        w_lo = [R[:, 9216:10240], R[:, 13312:14336], R[:, 11264:12288], R[:, 15360:16384]]
        qk_hi, qk_lo = cut(R, 16384, 2, 512), cut(R, 17408, 2, 512)
        pT_hi, pT_lo = cut(R, 18432, HB, P), cut(R, 18944, HB, P)
        f_hi, f_lo = R[:, 0:CHUNK], R[:, CHUNK:2 * CHUNK]
        h_hi, h_lo = R[:, 3072:4096], R[:, 4096:5120]

        rawT, rawC = cut(RAW1, 0, DC, T), cut(RAW2, 0, B, D)
        madd = cut(RAW2, 0, B, P)
        bm = [cut(RAW2, 1024, HB, P), cut(RAW2, 1536, HB, P)]
        S2 = cut(RAW2, 2048, HB, P)
        E = cut(RAW2, 2560, HB, P)
        bias_t = cut(RAW2, 3072, 2, P)
        mask8 = RAW2[:, 3328:3584].bitcast(U8).rearrange("p (b k) -> p b k", b=B)
        sc0, sc1, eg = cut(RAW2, 2048, B, NE), cut(RAW2, 2560, B, NE), cut(RAW2, 1024, B, NE)
        e0 = XN
        hbuf = [RAW2[:, 0:512], RAW2[:, 512:1024]]
        fw = RAW1[:, 0:CHUNK + SHIFTS].bitcast(I32)
        fs = RAW1[:, 2048:2048 + CHUNK]

        ld_x = [sem("ld_x0"), sem("ld_x1")]
        ld_small, ld_ctxT, ld_ctx, ld_ab, ld_mask, ld_bias = (
            sem(n) for n in ("ld_small", "ld_ctxT", "ld_ctx", "ld_ab", "ld_mask", "ld_bias"))
        ld_w = [sem(f"ld_w{i}") for i in range(4)]
        ident_ready, const_hi, const_lo = sem("ident_ready"), sem("const_hi"), sem("const_lo")
        gates_ready = sem("gates_ready")
        stats_ready, rstd_ready, nmr_ready, xn_ready = (
            sem(n) for n in ("stats_ready", "rstd_ready", "nmr_ready", "xn_ready"))
        rms_in, rms_ready, y_ready = sem("rms_in"), sem("rms_ready"), sem("y_ready")
        filled = sem("filled")
        drained = sem("drained")
        hi0 = sem("hi0")
        max0, exp0, p_hi0 = sem("max0"), sem("exp0"), sem("p_hi0")
        gate_max, gate_exp, zg_ready = sem("gate_max"), sem("gate_exp"), sem("zg_ready")
        v0 = sem("v0")
        rsum_ready = sem("rsum_ready")
        mask_ready = sem("mask_ready")
        w_hi_s = [sem(f"w_hi{i}") for i in range(4)]
        w_ready = [sem(f"w_ready{i}") for i in range(4)]
        qk_done, qk_hi_s, qk_lo_s = sem("qk_done"), sem("qk_hi"), sem("qk_lo")
        sc_done, bm_ready, bm_free = sem("sc_done"), sem("bm_ready"), sem("bm_free")
        max_s, nmx_s, exp_s, rs_s, p_s = (sem(n) for n in ("max_s", "nmx_s", "exp_s", "rs_s", "p_s"))
        pt_done, pt_hi_s, pt_lo_s = sem("pt_done"), sem("pt_hi"), sem("pt_lo")
        pv_done, at_hi_s, at_lo_s = sem("pv_done"), sem("at_hi"), sem("at_lo")
        fill_done, v_hi_s, fill_free = sem("fill_done"), sem("v_hi"), sem("fill_free")
        ld_f, deq_s, f13_hi, f13_ready, f2_hi, f2_ready = (
            sem(n) for n in ("ld_f", "deq_s", "f13_hi", "f13_ready", "f2_hi", "f2_ready"))
        ab_done, silu_s, h_s, h_hi_s, h_lo_s = (
            sem(n) for n in ("ab_done", "silu_s", "h_s", "h_hi", "h_lo"))
        o_done, o_free = sem("o_done"), sem("o_free")
        stored = sem("stored")

        def grp(stage, b):
            return 1 + B * stage + b

        LAST0 = grp(LN3_T, B - 1)
        LN4 = LAST0 + 1

        block = stack.enter_context(nc.Block())

        @block.sync
        def _(sp):
            sp.dma_start(par[:], small).then_inc(ld_small, 16)
            sp.dma_start(wqr, wq_r).then_inc(ld_small, 16)
            sp.dma_start(kyT, keysT).then_inc(ld_small, 16)
            for h in range(2):
                sp.dma_start(X[:, HB * h:HB * h + HB, :],
                             x[HB * h:HB * h + HB].rearrange("b p d -> p b d")).then_inc(ld_x[h], 16)
            sp.dma_start(rawT, ctxT.rearrange("(c p) t -> p c t", p=P)).then_inc(ld_ctxT, 16)
            sp.dma_start(rawC, ctx.rearrange("b p d -> p b d")).then_inc(ld_ctx, 16)
            sp.wait_ge(const_lo, DC)
            sp.dma_start(RAW1[:, :], ab).then_inc(ld_ab, 16)
            sp.wait_ge(const_lo, 2 * DC)
            sp.dma_start(mask8, mask.rearrange("b q k -> q b k")).then_inc(ld_mask, 16)
            sp.dma_start(bias_t, bias[0]).then_inc(ld_bias, 16)
            sp.wait_ge(const_lo, 3 * DC)
            for k in (WV, QK0, QK1, WO):
                sp.dma_start(RAW1[:, k * BLK:(k + 1) * BLK],
                             weights[0, :, k * BLK:(k + 1) * BLK]).then_inc(ld_w[k], 16)
            with sp.Fori(1, PAIRS) as n:
                for k in (WV, QK0, QK1, WO):
                    sp.wait_ge(const_lo, 3 * DC)
                    sp.wait_ge(w_ready[k], n)
                    sp.dma_start(RAW1[:, k * BLK:(k + 1) * BLK],
                                 weights[bass.ds(n, 1), :, k * BLK:(k + 1) * BLK]).then_inc(ld_w[k], 16)
                sp.wait_ge(mask_ready, 1)
                sp.wait_ge(bm_ready, n * 4)
                sp.dma_start(bias_t, bias[bass.ds(n, 1)]).then_inc(ld_bias, 16)

            def load_chunk(j):
                sp.dma_start(fw, words[j]).then_inc(ld_f, 16)
                sp.dma_start(fs, scales[j]).then_inc(ld_f, 16)

            for k in range(4):
                sp.wait_ge(w_ready[k], PAIRS)
            load_chunk(0)
            with sp.Fori(1, HC) as j:
                sp.wait_ge(w_ready[WO], PAIRS)
                sp.wait_ge(f2_ready, j)
                load_chunk(bass.ds(j, 1))
            for b in range(B):
                sp.wait_ge(o_free, 4 + B * (HC - 1) + b + 1)
                sp.dma_start(out[b], X[:, b, :]).then_inc(stored, 16)
            sp.wait_ge(stored, 16 * B)

        @block.gpsimd
        def _(pool):
            pool.memset(ident[:], 0.0).then_inc(ident_ready, 1)
            pool.memset(mhalf[:], -0.5).then_inc(ident_ready, 1)
            pool.wait_ge(ident_ready, 2)
            pool.affine_select(out=ident[:], in_=ident[:], compare_op=ALU.not_equal, fill=1.0, base=0,
                               pattern=[[-1, P]], channel_multiplier=1).then_inc(ident_ready, 1)

            def const_lows(first, hi, lo, raw):
                for c in range(DC):
                    pool.wait_ge(const_hi, first + c + 1)
                    pool.tensor_tensor(lo(c), raw(c), hi(c).bitcast(F32), ALU.subtract).then_inc(const_lo, 1)

            def inverse_root(n):
                pool.wait_ge(stats_ready, n)
                pool.tensor_tensor(rstd[:], vareps[:], mhalf[:], ALU.pow).then_inc(rstd_ready, 1)

            inverse_root(1)
            const_lows(0, lambda c: cT_hi[:, c, :], lambda c: cT_lo[:, c, :], lambda c: rawT[:, c, :])
            const_lows(DC, lambda c: c_hi[:, 2 * c:2 * c + 2, :], lambda c: c_lo[:, 2 * c:2 * c + 2, :],
                       lambda c: rawC[:, 2 * c:2 * c + 2, :])
            const_lows(2 * DC, ab_part(0), ab_part(1), lambda c: RAW1[:, c * 1024:(c + 1) * 1024])
            inverse_root(2)
            inverse_root(3)
            pool.wait_ge(rms_in, 1)
            pool.tensor_tensor(rms[:], vareps[:], mhalf[:], ALU.pow).then_inc(rms_ready, 1)

            pool.wait_ge(mask_ready, 1)
            pool.sem_inc(bm_free, 2)
            with pool.Fori(0, PAIRS) as i:
                pool.wait_ge(ld_bias, i * 16 + 16)
                for u in range(4):
                    h, t = u // 2, u % 2
                    pool.wait_ge(bm_free, i * 4 + (u + 1))
                    pool.tensor_tensor(bm[u % 2], madd[:, HB * t:HB * t + HB, :],
                                       bias_t[:, h:h + 1, :].broadcast_to([P, HB, P]),
                                       ALU.add).then_inc(bm_ready, 1)
            inverse_root(4)

        @block.scalar
        def _(act):
            def copy(o, i, **k):
                return act.activation(o, i, ACT.Copy, **k)

            act.wait_ge(ld_small, 48)
            act.activation(gate[:], par[:, 0:4], ACT.Tanh).then_inc(gates_ready, 1)
            act.wait_ge(ld_ctxT, 16)
            for c in range(DC):
                copy(cT_hi[:, c, :], rawT[:, c, :]).then_inc(const_hi, 1)

            def normalise(n):
                act.wait_ge(nmr_ready, n)
                for b in range(B):
                    act.activation(XN[:, b, :], X[:, b, :], ACT.Identity, bias=nmr[:, b:b + 1],
                                   scale=rstd[:, b:b + 1]).then_inc(xn_ready, 1)

            def hi_T(g, b, dst, n):
                act.wait_ge(filled, g + 1)
                copy(dst[:, :, b * P:(b + 1) * P], PS[g % 8][:].rearrange("p (c t) -> p c t", c=DC)
                     ).then_inc(hi0, 1)

            act.wait_ge(filled, 1)
            normalise(1)
            copy(g_hi, PS[0][:, 0:DC * NE].rearrange("p (c e) -> p c e", c=DC)).then_inc(hi0, 1)
            for b in range(B):
                hi_T(grp(LN1_T, b), b, xT_hi, 0)
            act.wait_ge(ld_ctx, 16)
            for c in range(DC):
                copy(c_hi[:, 2 * c:2 * c + 2, :], rawC[:, 2 * c:2 * c + 2, :]).then_inc(const_hi, 1)
            for b in range(B):
                act.wait_ge(max0, b + 1)
                act.activation(e0[:, b, 0:P], PS[grp(SIM, b) % 8][:, 0:P], ACT.Exp, bias=negmax[:, b:b + 1],
                               scale=float(P) ** -0.5, accum_out=esum[:, b:b + 1]).then_inc(exp0, 1)
            for b in range(B):
                act.wait_ge(rsum_ready, b + 1)
                copy(p_hi[:, b, :], e0[:, b, 0:P], scale=rsum[:, b:b + 1]).then_inc(p_hi0, 1)
            act.wait_ge(ld_ab, 16)
            for c in range(DC):
                copy(ab_part(0)(c), RAW1[:, c * 1024:(c + 1) * 1024]).then_inc(const_hi, 1)
            normalise(2)
            for b in range(B):
                hi_T(grp(LN2_T, b), b, xT_hi, 0)
            for b in range(B):
                act.wait_ge(gate_max, b + 1)
                act.activation(eg[:, b, :], sc0[:, b, :], ACT.Exp, bias=negmax[:, b:b + 1]).then_inc(gate_exp, 1)
            for b in range(B):
                hi_T(grp(GATED_T, b), b, zT_hi, 0)
            normalise(3)
            for b in range(B):
                act.wait_ge(filled, grp(LN3_T, b) + 1)
                for c in range(DC):
                    last = copy(xT_hi[:, c, b * P:(b + 1) * P],
                                PS[grp(LN3_T, b) % 8][:, c * P:(c + 1) * P], scale=par[:, 4 + c:5 + c])
                last.then_inc(hi0, 1)

            def weight_hi(k, n):
                act.wait_ge(ld_w[k], n * 16 + 16)
                copy(w_hi[k], RAW1[:, k * BLK:(k + 1) * BLK]).then_inc(w_hi_s[k], 1)

            def pair(i, more):
                def qk(u):
                    for s in range(2):
                        act.wait_ge(qk_done, i * 8 + (2 * u + s + 1))
                        copy(qk_hi[:, s, :], PS[s][:]).then_inc(qk_hi_s, 1)

                def value(n):
                    act.wait_ge(fill_done, i * 12 + (n + 1))
                    copy(v_hi[:, 2 * n:2 * n + 2, :], PS[5 + n % 3][:].rearrange("p (a b) -> p a b", a=2)
                         ).then_inc(v_hi_s, 1)

                def exps(u):
                    act.wait_ge(nmx_s, i * 4 + (u + 1))
                    for b in range(HB):
                        last = act.activation(E[:, b, :], S2[:, b, :], ACT.Exp, bias=u_nmx[:, b:b + 1],
                                              accum_out=u_sum[:, b:b + 1])
                    last.then_inc(exp_s, 1)

                def pT(u):
                    act.wait_ge(pt_done, i * 4 + (u + 1))
                    copy(pT_hi, PS[2][:].rearrange("p (a b) -> p a b", a=HB)).then_inc(pt_hi_s, 1)

                def attended(u):
                    act.wait_ge(pv_done, i * 4 + (u + 1))
                    copy(at_hi[:, u // 2, HALF * (u % 2):HALF * (u % 2) + HALF], PS[4][:]).then_inc(at_hi_s, 1)

                qk(0)
                value(0)
                value(1)
                exps(0)
                weight_hi(QK1, i)
                qk(1)
                pT(0)
                value(2)
                exps(1)
                attended(0)
                weight_hi(WO, i)
                qk(2)
                pT(1)
                value(3)
                exps(2)
                attended(1)
                if more:
                    weight_hi(WV, i + 1)
                qk(3)
                pT(2)
                exps(3)
                attended(2)
                if more:
                    weight_hi(QK0, i + 1)
                pT(3)
                attended(3)

            act.wait_ge(filled, grp(EXPERTS, B - 1) + 1)
            weight_hi(WV, 0)
            weight_hi(QK0, 0)
            with act.Fori(0, PAIRS - 1) as i:
                pair(i, True)
            pair(PAIRS - 1, False)

            act.wait_ge(nmr_ready, 4)
            normalise(4)
            for b in range(B):
                hi_T(LN4 + b, b, xT_hi, 0)

            def split_13(n):
                act.wait_ge(deq_s, n * 7 + 7)
                copy(f_hi[:, 0:2 * DC * P], fs[:, 0:2 * DC * P]).then_inc(f13_hi, 1)

            def split_2(n):
                copy(f_hi[:, 2 * DC * P:CHUNK], fs[:, 2 * DC * P:CHUNK]).then_inc(f2_hi, 1)

            def chunk(j, more):
                for t in range(2):
                    act.wait_ge(ab_done, j * 4 + (2 * t + 1))
                    act.activation(hbuf[t], PS[2 * t][:], ACT.Silu).then_inc(silu_s, 1)
                    act.wait_ge(h_s, j * 2 + (t + 1))
                    copy(h_hi[:, HALF * t:HALF * t + HALF], hbuf[t]).then_inc(h_hi_s, 1)
                if more:
                    act.wait_ge(ab_done, j * 4 + 4)
                    split_13(j + 1)
                    act.wait_ge(o_done, j * 8 + 8)
                    split_2(j + 1)

            split_13(0)
            split_2(0)
            with act.Fori(0, HC - 1) as j:
                chunk(j, True)
            chunk(HC - 1, False)

        @block.vector
        def _(dve):
            own = [0]

            def step(ins):
                own[0] += 1
                return ins.then_inc(v0, 1)

            def settle():
                dve.wait_ge(v0, own[0])

            def sub(o, a, b):
                return dve.tensor_tensor(o, a, b.bitcast(F32), ALU.subtract)

            his = [0]

            def lo_T(g, b, hi, lo):
                his[0] += 1
                dve.wait_ge(hi0, his[0])
                sub(lo[:, :, b * P:(b + 1) * P], PS[g % 8][:].rearrange("p (c t) -> p c t", c=DC),
                    hi[:, :, b * P:(b + 1) * P]).then_inc(drained, 1)

            def norm(n):
                settle()
                for b in range(B):
                    if n == 1 and b % HB == 0:
                        dve.wait_ge(ld_x[b // HB], 16)
                    step(dve.bn_stats(stat[:, b, :], X[:, b, :]))
                settle()
                for b in range(B):
                    step(dve.bn_aggr(mv[:, b, :], stat[:, b, :]))
                settle()
                dve.tensor_scalar(vareps[:], mv[:, :, 1], EPS, None, ALU.add).then_inc(stats_ready, 1)
                dve.wait_ge(rstd_ready, n)
                dve.scalar_tensor_tensor(nmr[:], mv[:, :, 0], -1.0, rstd[:], ALU.mult, ALU.mult
                                         ).then_inc(nmr_ready, 1)

            norm(1)
            dve.wait_ge(hi0, 1)
            his[0] = 1
            sub(g_lo, PS[0][:, 0:DC * NE].rearrange("p (c e) -> p c e", c=DC), g_hi).then_inc(drained, 1)
            for b in range(B):
                lo_T(grp(LN1_T, b), b, xT_hi, xT_lo)
            scale0 = float(P) ** -0.5
            for b in range(B):
                dve.wait_ge(filled, grp(SIM, b) + 1)
                step(dve.tensor_reduce(esum[:, b:b + 1], PS[grp(SIM, b) % 8][:, 0:P], AX.X, ALU.max))
                settle()
                dve.tensor_scalar(negmax[:, b:b + 1], esum[:, b:b + 1], -scale0, None, ALU.mult).then_inc(max0, 1)
            for b in range(B):
                dve.wait_ge(exp0, b + 1)
                dve.reciprocal(rsum[:, b:b + 1], esum[:, b:b + 1]).then_inc(rsum_ready, 1)
            for b in range(B):
                dve.wait_ge(rsum_ready, b + 1)
                dve.wait_ge(p_hi0, b + 1)
                dve.scalar_tensor_tensor(p_lo[:, b, :], e0[:, b, 0:P], rsum[:, b:b + 1],
                                         p_hi[:, b, :].bitcast(F32), ALU.mult, ALU.subtract
                                         ).then_inc(drained, 1)
            dve.wait_ge(gates_ready, 1)

            def add_in(g, b, k):
                dve.wait_ge(filled, g + 1)
                dve.scalar_tensor_tensor(X[:, b, :], PS[g % 8][:], gate[:, k:k + 1], X[:, b, :],
                                         ALU.mult, ALU.add).then_inc(drained, 1)

            for b in range(B):
                add_in(grp(CONTEXT, b), b, 0)
            dve.wait_ge(drained, grp(CONTEXT, B - 1) + 1)
            norm(2)
            for b in range(B):
                lo_T(grp(LN2_T, b), b, xT_hi, xT_lo)
            dve.wait_ge(const_lo, 2 * DC)
            for b in range(B):
                dve.wait_ge(filled, grp(ROUTE, b) + 1)
                dve.tensor_copy(sc0[:, b, :], PS[grp(ROUTE, b) % 8][:, 0:NE]).then_inc(drained, 1)
            dve.wait_ge(drained, grp(ROUTE, B - 1) + 1)
            for b in range(B):
                step(dve.max(top[:, b, 0:8], sc0[:, b, :]))
            settle()
            for b in range(B):
                dve.tensor_scalar(negmax[:, b:b + 1], top[:, b, 0:1], -1.0, None, ALU.mult).then_inc(gate_max, 1)
            for b in range(B):
                step(dve.match_replace(sc1[:, b, :], top[:, b, 0:8], sc0[:, b, :], LOWEST))
            settle()
            for b in range(B):
                step(dve.max(top[:, b, 8:16], sc1[:, b, :]))
            settle()
            for b in range(B):
                step(dve.match_replace(sc1[:, b, :], top[:, b, 8:16], sc1[:, b, :], LOWEST))
            settle()
            dve.wait_ge(gate_exp, B)
            for b in range(B):
                step(dve.scalar_tensor_tensor(eg[:, b, :], sc1[:, b, :], TAKEN, eg[:, b, :], ALU.is_le,
                                              ALU.mult, accum_out=esum[:, b:b + 1]))
            settle()
            step(dve.reciprocal(rsum[:], esum[:]))
            settle()
            for b in range(B):
                step(dve.tensor_scalar(eg[:, b, :], eg[:, b, :], rsum[:, b:b + 1], LORA_SCALE, ALU.mult, ALU.mult))
            settle()
            for b in range(B):
                dve.wait_ge(filled, grp(EXPERTS, b) + 1)
                dve.tensor_tensor(XN[:, b, :].rearrange("p (e r) -> p e r", e=NE),
                                  PS[grp(EXPERTS, b) % 8][:].rearrange("p (e r) -> p e r", e=NE),
                                  eg[:, b, :].rearrange("p (e o) -> p e o", o=1).broadcast_to([P, NE, RANK]),
                                  ALU.mult).then_inc(drained, 1)
            for b in range(B):
                lo_T(grp(GATED_T, b), b, zT_hi, zT_lo)
            for b in range(B):
                add_in(grp(MIX, b), b, 2)
            dve.wait_ge(drained, grp(MIX, B - 1) + 1)
            norm(3)
            settle()
            dve.wait_ge(nmr_ready, 3)
            step(dve.tensor_tensor(vareps[:], mv[:, :, 1], rstd[:], ALU.mult))
            settle()
            step(dve.tensor_tensor(vareps[:], vareps[:], rstd[:], ALU.mult))
            settle()
            dve.tensor_scalar(vareps[:], vareps[:], EPS, None, ALU.add).then_inc(rms_in, 1)
            for b in range(B):
                dve.wait_ge(xn_ready, 2 * B + b + 1)
                step(dve.scalar_tensor_tensor(X[:, b, :], XN[:, b, :], gate[:, 1:2], X[:, b, :],
                                              ALU.mult, ALU.add))
            settle()
            dve.wait_ge(rms_ready, 1)
            for b in range(B):
                dve.tensor_scalar(XN[:, b, :], XN[:, b, :], rms[:, b:b + 1], None, ALU.mult).then_inc(y_ready, 1)
            dve.wait_ge(ld_mask, 16)
            dve.tensor_scalar(madd, mask8, -1.0, FAR, ALU.add, ALU.mult).then_inc(mask_ready, 1)
            step(dve.tensor_reduce(keep[:], mask8, AX.X, ALU.max))
            for b in range(B):
                g = grp(LN3_T, b)
                his[0] += 1
                dve.wait_ge(hi0, his[0])
                for c in range(DC):
                    last = dve.scalar_tensor_tensor(xT_lo[:, c, b * P:(b + 1) * P], PS[g % 8][:, c * P:(c + 1) * P],
                                                    par[:, 4 + c:5 + c],
                                                    xT_hi[:, c, b * P:(b + 1) * P].bitcast(F32),
                                                    ALU.mult, ALU.subtract)
                last.then_inc(drained, 1)
            settle()

            def weight_lo(k, n):
                dve.wait_ge(w_hi_s[k], n + 1)
                sub(w_lo[k], RAW1[:, k * BLK:(k + 1) * BLK], w_hi[k]).then_inc(w_ready[k], 1)

            def pair(i, more):
                def qk(u):
                    for s in range(2):
                        dve.wait_ge(qk_hi_s, i * 8 + (2 * u + s + 1))
                        sub(qk_lo[:, s, :], PS[s][:], qk_hi[:, s, :]).then_inc(qk_lo_s, 1)

                def value(n):
                    dve.wait_ge(v_hi_s, i * 4 + (n + 1))
                    sub(v_lo[:, 2 * n:2 * n + 2, :], PS[5 + n % 3][:].rearrange("p (a b) -> p a b", a=2),
                        v_hi[:, 2 * n:2 * n + 2, :]).then_inc(fill_free, 1)

                def maxima(u):
                    dve.wait_ge(mask_ready, 1)
                    dve.wait_ge(sc_done, i * 4 + (u + 1))
                    dve.wait_ge(bm_ready, i * 4 + (u + 1))
                    for b in range(HB):
                        dve.tensor_tensor_reduce(S2[:, b, :], PS[3][:, b * P:(b + 1) * P], bm[u % 2][:, b, :],
                                                 1.0, LOWEST, ALU.add, ALU.max, u_max[:, b:b + 1]
                                                 ).then_inc(max_s, 1)
                    dve.wait_ge(max_s, i * 16 + (4 * u + 4))
                    dve.tensor_scalar(u_nmx[:], u_max[:], -1.0, None, ALU.mult).then_inc(nmx_s, 1)

                def normed(u):
                    t = u % 2
                    dve.wait_ge(exp_s, i * 4 + (u + 1))
                    dve.reciprocal(u_rs[:], u_sum[:]).then_inc(rs_s, 1)
                    dve.wait_ge(rs_s, i * 8 + (2 * u + 1))
                    dve.tensor_tensor(u_rs[:], u_rs[:], keep[:, HB * t:HB * t + HB], ALU.mult).then_inc(rs_s, 1)
                    dve.wait_ge(rs_s, i * 8 + (2 * u + 2))
                    dve.tensor_tensor(E, E, u_rs[:].rearrange("p (a o) -> p a o", o=1).broadcast_to([P, HB, P]),
                                      ALU.mult).then_inc(p_s, 1)
                    dve.sem_inc(bm_free, 1)

                def pT(u):
                    dve.wait_ge(pt_hi_s, i * 4 + (u + 1))
                    sub(pT_lo, PS[2][:].rearrange("p (a b) -> p a b", a=HB), pT_hi).then_inc(pt_lo_s, 1)

                def attended(u):
                    at = slice(HALF * (u % 2), HALF * (u % 2) + HALF)
                    dve.wait_ge(at_hi_s, i * 4 + (u + 1))
                    sub(at_lo[:, u // 2, at], PS[4][:], at_hi[:, u // 2, at]).then_inc(at_lo_s, 1)

                def add_out(n):
                    dve.wait_ge(fill_done, i * 12 + (4 + n + 1))
                    dve.scalar_tensor_tensor(X[:, n, :], PS[5 + (4 + n) % 3][:], gate[:, 1:2], X[:, n, :],
                                             ALU.mult, ALU.add).then_inc(fill_free, 1)

                qk(0)
                value(0)
                value(1)
                maxima(0)
                normed(0)
                weight_lo(QK1, i)
                qk(1)
                pT(0)
                value(2)
                maxima(1)
                normed(1)
                attended(0)
                weight_lo(WO, i)
                qk(2)
                pT(1)
                value(3)
                maxima(2)
                attended(1)
                normed(2)
                if more:
                    weight_lo(WV, i + 1)
                qk(3)
                pT(2)
                maxima(3)
                attended(2)
                normed(3)
                if more:
                    weight_lo(QK0, i + 1)
                for n in range(4):
                    add_out(n)
                pT(3)
                attended(3)
                for n in range(4, 8):
                    add_out(n)

            weight_lo(WV, 0)
            weight_lo(QK0, 0)
            with dve.Fori(0, PAIRS - 1) as i:
                pair(i, True)
            pair(PAIRS - 1, False)

            dve.wait_ge(fill_free, 3 + 12 * PAIRS)
            norm(4)
            for b in range(B):
                lo_T(LN4 + b, b, xT_hi, xT_lo)

            def dequantise(n):
                dve.wait_ge(ld_f, n * 32 + 32)
                W13 = slice(0, 2 * DC * P)
                w2 = fw[:, 2 * DC * P:CHUNK].rearrange("p (m r) -> p r m", r=4)
                for k in range(5):
                    part = fw[:, W13] if k == 0 else w2[:, k - 1, :]
                    s = CHUNK + 2 * k
                    dve.tensor_scalar(part, part, fw[:, s:s + 1], fw[:, s + 1:s + 2],
                                      ALU.logical_shift_left, ALU.arith_shift_right).then_inc(deq_s, 1)
                dve.wait_ge(deq_s, n * 7 + 5)
                dve.tensor_tensor(fs[:, W13], fw[:, W13], fs[:, W13], ALU.mult).then_inc(deq_s, 1)
                dve.tensor_tensor(fs[:, 2 * DC * P:CHUNK], fw[:, 2 * DC * P:CHUNK], fs[:, 2 * DC * P:CHUNK],
                                  ALU.mult).then_inc(deq_s, 1)

            def lows_13(n):
                dve.wait_ge(f13_hi, n + 1)
                sub(f_lo[:, 0:2 * DC * P], fs[:, 0:2 * DC * P], f_hi[:, 0:2 * DC * P]).then_inc(f13_ready, 1)

            def lows_2(n):
                dve.wait_ge(f2_hi, n + 1)
                sub(f_lo[:, 2 * DC * P:CHUNK], fs[:, 2 * DC * P:CHUNK], f_hi[:, 2 * DC * P:CHUNK]
                    ).then_inc(f2_ready, 1)

            def hidden(j, t):
                dve.wait_ge(silu_s, j * 2 + (t + 1))
                dve.wait_ge(ab_done, j * 4 + (2 * t + 2))
                dve.tensor_tensor(hbuf[t], PS[2 * t + 1][:], hbuf[t], ALU.mult).then_inc(h_s, 1)

            def hidden_lo(j, t):
                dve.wait_ge(h_hi_s, j * 2 + (t + 1))
                at = slice(HALF * t, HALF * t + HALF)
                sub(h_lo[:, at], hbuf[t], h_hi[:, at]).then_inc(h_lo_s, 1)

            def chunk(j, more):
                hidden(j, 0)
                hidden_lo(j, 0)
                if more:
                    dequantise(j + 1)
                hidden(j, 1)
                hidden_lo(j, 1)
                if more:
                    lows_13(j + 1)
                for n in range(B):
                    dve.wait_ge(o_done, j * 8 + (n + 1))
                    dve.scalar_tensor_tensor(X[:, n, :], PS[4 + n % 4][:], gate[:, 3:4], X[:, n, :],
                                             ALU.mult, ALU.add).then_inc(o_free, 1)
                if more:
                    lows_2(j + 1)

            dequantise(0)
            lows_13(0)
            lows_2(0)
            with dve.Fori(0, HC - 1) as j:
                chunk(j, True)
            chunk(HC - 1, False)

        @block.tensor
        def _(pe):
            def split_mm(o, wh, wl, mh, ml, first, last):
                pe.matmul(o, wh, mh, start=first, stop=False)
                pe.matmul(o, wh, ml, start=False, stop=False)
                return pe.matmul(o, wl, mh, start=False, stop=last)

            def claim(g):
                if g >= 8:
                    pe.wait_ge(drained, g - 7)
                return PS[g % 8]

            def transpose_tile(g, b):
                ps = claim(g)
                for c in range(DC):
                    last = pe.transpose(ps[:, c * P:(c + 1) * P], XN[:, b, c * P:(c + 1) * P], ident[:])
                last.then_inc(filled, 1)

            pe.wait_ge(ld_small, 48)
            for c in range(DC):
                last = pe.matmul(PS[0][:, c * NE:(c + 1) * NE], wqr[:, c * P:(c + 1) * P], kyT,
                                 start=True, stop=True)
            last.then_inc(filled, 1)
            pe.wait_ge(ident_ready, 3)
            for b in range(B):
                pe.wait_ge(xn_ready, b + 1)
                transpose_tile(grp(LN1_T, b), b)
            pe.wait_ge(const_lo, DC)
            for b in range(B):
                pe.wait_ge(drained, grp(LN1_T, b) + 1)
                ps = claim(grp(SIM, b))
                t = slice(b * P, (b + 1) * P)
                for c in range(DC):
                    last = split_mm(ps[:, 0:P], xT_hi[:, c, t], xT_lo[:, c, t], cT_hi[:, c, t], cT_lo[:, c, t],
                                    c == 0, c == DC - 1)
                last.then_inc(filled, 1)
            pe.wait_ge(const_lo, 2 * DC)
            for b in range(B):
                pe.wait_ge(drained, grp(SIM, b) + 1)
                ps = claim(grp(CONTEXT, b))
                split_mm(ps[:], p_hi[:, b, :], p_lo[:, b, :], c_hi[:, b, :], c_lo[:, b, :], True, True
                         ).then_inc(filled, 1)
            for b in range(B):
                pe.wait_ge(xn_ready, B + b + 1)
                transpose_tile(grp(LN2_T, b), b)
            for b in range(B):
                pe.wait_ge(drained, grp(LN2_T, b) + 1)
                ps = claim(grp(ROUTE, b))
                t = slice(b * P, (b + 1) * P)
                for c in range(DC):
                    last = split_mm(ps[:, 0:NE], xT_hi[:, c, t], xT_lo[:, c, t], g_hi[:, c, :], g_lo[:, c, :],
                                    c == 0, c == DC - 1)
                last.then_inc(filled, 1)
            pe.wait_ge(const_lo, 3 * DC)
            for b in range(B):
                ps = claim(grp(EXPERTS, b))
                t = slice(b * P, (b + 1) * P)
                for c in range(DC):
                    last = split_mm(ps[:], xT_hi[:, c, t], xT_lo[:, c, t], a_hi[:, c, :], a_lo[:, c, :],
                                    c == 0, c == DC - 1)
                last.then_inc(filled, 1)
            for b in range(B):
                pe.wait_ge(drained, grp(EXPERTS, b) + 1)
                transpose_tile(grp(GATED_T, b), b)
            for b in range(B):
                pe.wait_ge(drained, grp(GATED_T, b) + 1)
                ps = claim(grp(MIX, b))
                t = slice(b * P, (b + 1) * P)
                for c in range(DC):
                    last = split_mm(ps[:], zT_hi[:, c, t], zT_lo[:, c, t], b_hi[:, c, :], b_lo[:, c, :],
                                    c == 0, c == DC - 1)
                last.then_inc(filled, 1)
            for b in range(B):
                pe.wait_ge(y_ready, b + 1)
                transpose_tile(grp(LN3_T, b), b)
            pe.wait_ge(drained, LAST0 + 1)

            pe.sem_inc(fill_free, 3)
            with pe.Fori(0, PAIRS) as i:
                def project(u, s):
                    hi, lo = (xT_hi, xT_lo) if s == 0 else (cT_hi, cT_lo)
                    t = slice(HALF * (u % 2), HALF * (u % 2) + HALF)
                    for c in range(DC):
                        w = slice((s * DC + c) * P, (s * DC + c + 1) * P)
                        last = split_mm(PS[s][:], w_hi[u // 2][:, w], w_lo[u // 2][:, w], hi[:, c, t], lo[:, c, t],
                                        c == 0, c == DC - 1)
                    last.then_inc(qk_done, 1)

                def values(n):
                    pe.wait_ge(fill_free, i * 12 + (n + 1))
                    for a in range(2):
                        t = slice((2 * n + a) * P, (2 * n + a + 1) * P)
                        for c in range(DC):
                            w = slice(c * 256, (c + 1) * 256)
                            last = split_mm(PS[5 + n % 3][:, a * 256:(a + 1) * 256], cT_hi[:, c, t], cT_lo[:, c, t],
                                            w_hi[WV][:, w], w_lo[WV][:, w], c == 0, c == DC - 1)
                    last.then_inc(fill_done, 1)

                def scores(u):
                    pe.wait_ge(qk_lo_s, i * 8 + (2 * u + 2))
                    for b in range(HB):
                        t = slice(b * P, (b + 1) * P)
                        last = split_mm(PS[3][:, t], qk_hi[:, 0, t], qk_lo[:, 0, t], qk_hi[:, 1, t], qk_lo[:, 1, t],
                                        True, True)
                    last.then_inc(sc_done, 1)

                def transpose_p(u):
                    pe.wait_ge(p_s, i * 4 + (u + 1))
                    for b in range(HB):
                        last = pe.transpose(PS[2][:, b * P:(b + 1) * P], E[:, b, :], ident[:])
                    last.then_inc(pt_done, 1)

                def attend(u):
                    pe.wait_ge(pt_lo_s, i * 4 + (u + 1))
                    if u < 2:
                        pe.wait_ge(fill_free, i * 12 + (3 + 2 * u + 2))
                    if u > 0:
                        pe.wait_ge(at_lo_s, i * 4 + u)
                    h = u // 2
                    for b in range(HB):
                        n = HB * (u % 2) + b
                        v = slice(h * DH, (h + 1) * DH)
                        last = split_mm(PS[4][:, b * P:(b + 1) * P], v_hi[:, n, v], v_lo[:, n, v],
                                        pT_hi[:, b, :], pT_lo[:, b, :], True, True)
                    last.then_inc(pv_done, 1)

                def project_out(n, h):
                    ps = PS[5 + (4 + n) % 3]
                    if h == 0:
                        pe.wait_ge(fill_free, i * 12 + (4 + n + 1))
                    t = slice(n * P, (n + 1) * P)
                    w = slice(h * D, (h + 1) * D)
                    last = split_mm(ps[:], at_hi[:, h, t], at_lo[:, h, t], w_hi[WO][:, w], w_lo[WO][:, w],
                                    h == 0, h == 1)
                    if h == 1:
                        last.then_inc(fill_done, 1)

                pe.wait_ge(w_ready[QK0], i + 1)
                project(0, 0)
                project(0, 1)
                pe.wait_ge(w_ready[WV], i + 1)
                values(0)
                values(1)
                scores(0)
                project(1, 0)
                project(1, 1)
                transpose_p(0)
                values(2)
                scores(1)
                attend(0)
                pe.wait_ge(w_ready[QK1], i + 1)
                project(2, 0)
                project(2, 1)
                transpose_p(1)
                values(3)
                scores(2)
                attend(1)
                project(3, 0)
                project(3, 1)
                transpose_p(2)
                pe.wait_ge(w_ready[WO], i + 1)
                project_out(0, 0)
                project_out(1, 0)
                scores(3)
                attend(2)
                project_out(2, 0)
                pe.wait_ge(at_lo_s, i * 4 + 3)
                for n in range(3):
                    project_out(n, 1)
                project_out(3, 0)
                project_out(3, 1)
                transpose_p(3)
                project_out(4, 0)
                project_out(5, 0)
                attend(3)
                project_out(6, 0)
                pe.wait_ge(at_lo_s, i * 4 + 4)
                for n in range(4, 7):
                    project_out(n, 1)
                project_out(7, 0)
                project_out(7, 1)

            pe.wait_ge(fill_free, 3 + 12 * PAIRS)
            for b in range(B):
                pe.wait_ge(xn_ready, 3 * B + b + 1)
                transpose_tile(LN4 + b, b)
            pe.wait_ge(drained, LN4 + B)
            pe.sem_inc(o_free, 4)
            with pe.Fori(0, HC) as j:
                pe.wait_ge(f13_ready, j + 1)
                for t in range(2):
                    at = slice(HALF * t, HALF * t + HALF)
                    for m in range(2):
                        for c in range(DC):
                            w = slice((m * DC + c) * P, (m * DC + c + 1) * P)
                            last = split_mm(PS[2 * t + m][:], f_hi[:, w], f_lo[:, w], xT_hi[:, c, at],
                                            xT_lo[:, c, at], c == 0, c == DC - 1)
                        last.then_inc(ab_done, 1)
                pe.wait_ge(f2_ready, j + 1)
                for n in range(B):
                    if n % HB == 0:
                        pe.wait_ge(h_lo_s, j * 2 + (n // HB + 1))
                    pe.wait_ge(o_free, j * 8 + (n + 1))
                    t = slice(n * P, (n + 1) * P)
                    w = slice(2 * DC * P, CHUNK)
                    split_mm(PS[4 + n % 4][:], h_hi[:, t], h_lo[:, t], f_hi[:, w], f_lo[:, w], True, True
                             ).then_inc(o_done, 1)


def _layouts(np, a):
    f = np.ascontiguousarray
    ctx = a["ctx_4096"]
    small = np.zeros((P, 8), np.float32)
    small[:, 0:2] = a["g_xattn"]
    small[:, 2:4] = a["g_ffn"]
    small[:, 4:8] = a["L1_xattn_ln_weight"].reshape(DC, P).T
    by_width = lambda w: w.T.reshape(DC, P, -1).transpose(1, 0, 2)
    ab = np.concatenate([by_width(a["L0_ffn_A_w"]).reshape(P, -1), by_width(a["L0_ffn_B_w"]).reshape(P, -1)], 1)
    q, k, v = (by_width(a[f"L1_xattn_w_{n}"]).reshape(P, DC, PAIRS, 2, DH) for n in "qkv")
    weights = np.empty((PAIRS, P, 4, BLK), np.float32)
    for h in range(2):
        qk = np.stack([q[:, :, :, h], k[:, :, :, h]])
        weights[:, :, QK0 + h] = qk.transpose(3, 1, 0, 2, 4).reshape(PAIRS, P, BLK)
    weights[:, :, WV] = v.transpose(2, 0, 1, 3, 4).reshape(PAIRS, P, BLK)
    o = a["L1_xattn_w_out"].T.reshape(PAIRS, 2, DH, D)
    weights[:, :, WO] = o.transpose(0, 2, 1, 3).reshape(PAIRS, P, BLK)
    bias = a["L1_xattn_position_bias"].reshape(PAIRS, 2, P, P).transpose(0, 2, 1, 3)

    def spread(packed, s, rows, cols):
        n = np.arange(rows * cols).reshape(rows, cols)
        return packed[n // 128, n % 64].T, s[n // 64].T

    words = np.zeros((HC, P, CHUNK + SHIFTS), np.int32)
    scales = np.zeros((HC, P, CHUNK), np.float32)

    def hidden_chunks(m):
        m = np.pad(m, ((0, 0), (0, HC * P - HID)))
        return m.reshape(DC, P, HC, P).transpose(2, 1, 0, 3).reshape(HC, P, DC * P)

    for at, n in ((0, "1"), (DC * P, "3")):
        w, s = spread(a[f"L1_ffn_w{n}"], a[f"L1_ffn_s{n}"], HID, D)
        words[:, :, at:at + DC * P] = hidden_chunks(w)
        scales[:, :, at:at + DC * P] = hidden_chunks(s)
    w, s = spread(a["L1_ffn_w2"], a["L1_ffn_s2"], D, HID)
    words[:, :, 2 * DC * P:CHUNK] = np.pad(w, ((0, HC * P - HID), (0, 0))).reshape(HC, P, D)
    scales[:, :, 2 * DC * P:] = np.pad(s, ((0, HC * P - HID), (0, 0))).reshape(HC, P, D)
    low13 = (np.arange(P) // 64 % 2)[None, :, None]
    hid = np.arange(HC * P).reshape(HC, P)
    low2 = (hid[:, :, None] + HID * np.arange(4)) // 64 % 2
    low = np.concatenate([np.broadcast_to(low13, (HC, P, 1)), low2], 2)
    words[:, :, CHUNK:] = np.stack([28 * low, 4 + 24 * low], 3).reshape(HC, P, SHIFTS)
    return {
        "x": f(a["x"]), "ctx": f(ctx), "ctxT": f(ctx.reshape(T, D).T),
        "mask": f(a["mask_BxSxS2_bk0"]), "small": small,
        "wq_r": f(a["L0_ffn_Wq_w"]), "keysT": f(a["L0_ffn_keys"].T), "ab": f(ab),
        "weights": f(weights.reshape(PAIRS, P, 4 * BLK)), "bias": f(bias),
        "words": words, "scales": scales,
    }


def kernel(**inputs):
    import numpy as np
    from concourse import bacc
    from concourse.bass_utils import run_bass_kernel_spmd

    arrays = _layouts(np, {k: np.asarray(v) for k, v in inputs.items()})
    nc = bacc.Bacc("TRN2", target_bir_lowering=False, num_devices=1)
    aps = {k: nc.dram_tensor(f"in_{k}", v.shape, mybir.dt.from_np(v.dtype), kind="ExternalInput").ap()
           for k, v in arrays.items()}
    out = nc.dram_tensor("out_x", (B, P, D), F32, kind="ExternalOutput").ap()
    gated_layers(nc, out=out, **aps)
    result = run_bass_kernel_spmd(nc, [{f"in_{k}": v for k, v in arrays.items()}], core_ids=[0])
    return result.results[0]["out_x"]
```

```python
from contextlib import ExitStack

import concourse.bass as bass
import concourse.mybir as mybir

F32 = mybir.dt.float32
F32R = mybir.dt.float32r
I32 = mybir.dt.int32
U8 = mybir.dt.uint8
ALU = mybir.AluOpType
ACT = mybir.ActivationFunctionType
AX = mybir.AxisListType

P = 128
B = 8
D = 512
DC = D // P
T = B * P
HALF = T // 2
HB = B // 2
NE, RANK, TOPK, RD = 64, 8, 16, 16
LORA_SCALE = 32 / TOPK
HEADS, DH = 32, 128
PAIRS = HEADS // 2
HID = 1376
HC = (HID + P - 1) // P
CHUNK = 2 * DC * P + D
SHIFTS = 10
EPS = 1e-5
FAR = 1e30
LOWEST = -3.0e38
TAKEN = -1.0e38

QK0, QK1, WV, WO = range(4)
BLK = 1024
(LN1_T, SIM, CONTEXT, LN2_T, ROUTE, EXPERTS, GATED_T, MIX, LN3_T) = range(9)
ORDER = [(LN1_T, 0), (LN1_T, 1), (SIM, 0), (SIM, 1), (CONTEXT, 0), (CONTEXT, 1), (LN2_T, 0), (ROUTE, 0),
         (LN2_T, 1), (ROUTE, 1), (EXPERTS, 0), (EXPERTS, 1), (GATED_T, 0), (GATED_T, 1), (MIX, 0),
         (MIX, 1), (LN3_T, 0), (LN3_T, 1)]


def gated_layers(nc, x, ctx, ctxT, mask, small, norm_w, wq_r, keysT, ab, weights, bias, words, scales, out):
    with ExitStack() as stack:
        def sb(name, shape, dt=F32):
            return stack.enter_context(nc.sbuf_tensor(name, shape, dt))

        def sem(name):
            return stack.enter_context(nc.semaphore(name))

        psum = stack.enter_context(nc.psum_tensor("psum", [P, 8, 512], F32))
        PS = [psum[:, i, :] for i in range(8)]

        X = sb("X", [P, B, D])
        XN = sb("XN", [P, B, D])
        xT_hi = sb("xT_hi", [P, DC, T], F32R)
        xT_lo = sb("xT_lo", [P, DC, T], F32R)
        cT = sb("cT", [P, 2, DC, T], F32R)
        cT_hi, cT_lo = cT[:, 0], cT[:, 1]
        RAW1 = sb("RAW1", [P, 4096])
        RAW2 = sb("RAW2", [P, 4096])
        R = sb("R", [P, 19456], F32R)

        ident = sb("ident", [P, P])
        par = sb("par", [P, 4])
        gate = sb("gate", [P, 4])
        wqr, kyT = XN[0:RD, 6, :], XN[0:RD, 7, 0:NE]
        stat = sb("stat", [P, B, 6])
        mv = sb("mv", [P, B, 2])
        vareps = sb("vareps", [P, B])
        mhalf = sb("mhalf", [P, B])
        rstd = sb("rstd", [P, B])
        nmr = sb("nmr", [P, B])
        rms = sb("rms", [P, B])
        negmax = sb("negmax", [P, B])
        esum = sb("esum", [P, B])
        rsum = sb("rsum", [P, B])
        top = sb("top", [P, B, 16])
        keep = sb("keep", [P, B])
        u_max = sb("u_max", [P, HB])
        u_nmx = sb("u_nmx", [P, HB])
        u_sum = sb("u_sum", [P, HB])
        u_rs = sb("u_rs", [P, HB])

        def cut(t, at, *dims):
            n = 1
            for d in dims:
                n *= d
            v = t[:, at:at + n]
            if len(dims) == 2:
                v = v.rearrange("p (a b) -> p a b", a=dims[0])
            if len(dims) == 3:
                v = v.rearrange("p (a b c) -> p a b c", a=dims[0], b=dims[1])
            return v

        c_hi, c_lo = cut(R, 0, B, D), cut(R, 4096, B, D)
        zT_hi, zT_lo = cut(R, 0, DC, T), cut(R, 4096, DC, T)
        a_hi, a_lo = cut(R, 8192, DC, D), cut(R, 10240, DC, D)
        b_hi, b_lo = cut(R, 12288, DC, D), cut(R, 14336, DC, D)
        p_hi, p_lo = cut(R, 16384, B, P), cut(R, 17408, B, P)
        g = cut(R, 18432, 2, DC, NE)
        g_hi, g_lo = g[:, 0], g[:, 1]
        def ab_part(half):
            def part(c):
                at = (8192, 12288)[c // 2] + 2048 * half + 1024 * (c % 2)
                return R[:, at:at + 1024]
            return part

        v_hi, v_lo = cut(R, 0, B, 256), cut(R, 2048, B, 256)
        at_hi, at_lo = cut(R, 4096, 2, T), cut(R, 6144, 2, T)
        w_hi = [R[:, 8192:9216], R[:, 12288:13312], R[:, 10240:11264], R[:, 14336:15360]]
        w_lo = [R[:, 9216:10240], R[:, 13312:14336], R[:, 11264:12288], R[:, 15360:16384]]
        q_hi, q_lo = R[:, 16384:16896], R[:, 16896:17408]
        kk = cut(R, 17408, HB, 2 * P)
        k_hi, k_lo = kk[:, :, 0:P], kk[:, :, P:2 * P]
        pp = cut(R, 18432, HB, 2 * P)
        pT_hi, pT_lo = pp[:, :, 0:P], pp[:, :, P:2 * P]
        sc = psum[:, 3:5, :].rearrange("p k (a w) -> p (k a) w", a=2)

        def unit(u):
            return u % 2, u // 2

        V_FILLS = {0: (0, 1), 2: (6, 7)}
        O_FILLS = {1: range(2, 6), 3: range(8, 12)}

        def place(i, k, first):
            if first and k < 2:
                return k
            return k - 6 if i is PAIRS else k - 4

        def fills(i, k, first):
            return i * 12 + (place(i, k, first) + 1)

        def fill_bank(i, k, first):
            return 5 + place(i, k, first) % 3

        def half(h):
            return range(HB * h, HB * h + HB)

        def hid_bank(t, m):
            return (2 * t + m + 1) % 4

        f_hi, f_lo = R[:, 8192:8192 + CHUNK], R[:, 8192 + CHUNK:8192 + 2 * CHUNK]
        h_hi, h_lo = R[:, 0:1024], R[:, 1024:2048]

        rawT, rawC = cut(RAW1, 0, DC, T), cut(RAW2, 0, B, D)
        madd = cut(RAW2, 0, B, P)
        bm = [cut(RAW2, 1024, HB, P), cut(RAW2, 1536, HB, P)]
        S2 = cut(RAW2, 2048, HB, P)
        E = cut(RAW2, 2560, HB, P)
        bias_t = cut(RAW2, 3072, 2, P)
        mask8 = RAW2[:, 3328:3584].bitcast(U8).rearrange("p (b k) -> p b k", b=B)
        sc0, sc1, eg = cut(RAW2, 2048, B, NE), cut(RAW2, 2560, B, NE), cut(RAW2, 1024, B, NE)
        e0, s0 = XN[:, :, 0:P], XN[:, :, P:2 * P]
        y0 = cut(RAW2, 1024, HB, D)
        hbuf = [RAW2[:, 2560:3072], RAW2[:, 0:512]]
        fw = RAW1[:, 0:CHUNK + SHIFTS].bitcast(I32)
        fs = RAW1[:, 2048:2048 + CHUNK]
        fd = RAW2[:, 1024:1024 + CHUNK]
        nw = RAW2[:, 3584:4096]

        ld_x = [sem("ld_x0"), sem("ld_x1")]
        ld_small, ld_ctxT, ld_ctx, ld_ab, ld_mask, ld_bias = (
            sem(n) for n in ("ld_small", "ld_ctxT", "ld_ctx", "ld_ab", "ld_mask", "ld_bias"))
        ld_w = [sem(f"ld_w{i}") for i in range(4)]
        ident_ready = sem("ident_ready")
        const_hi, const_hi_v, const_lo_v, const_lo = (
            sem(n) for n in ("const_hi", "const_hi_v", "const_lo_v", "const_lo"))
        gates_ready = sem("gates_ready")
        stats_ready, rstd_ready, nmr_ready, xn_ready = (
            sem(n) for n in ("stats_ready", "rstd_ready", "nmr_ready", "xn_ready"))
        rms_in, rms_ready, y_ready = sem("rms_in"), sem("rms_ready"), sem("y_ready")
        filled = sem("filled")
        drained = sem("drained")
        hi0 = sem("hi0")
        max0, exp0, p_hi0 = sem("max0"), sem("exp0"), sem("p_hi0")
        gate_max, gate_exp, zg_ready = sem("gate_max"), sem("gate_exp"), sem("zg_ready")
        v0 = sem("v0")
        rsum_ready = sem("rsum_ready")
        mask_ready = sem("mask_ready")
        w_hi_s = [sem(f"w_hi{i}") for i in range(4)]
        w_ready = [sem(f"w_ready{i}") for i in range(4)]
        qk_done, qk_hi_s, qk_lo_s = sem("qk_done"), sem("qk_hi"), sem("qk_lo")
        sc_done, bm_ready, bm_free = sem("sc_done"), sem("bm_ready"), sem("bm_free")
        bm_summed = sem("bm_summed")
        max_s, nmx_s, exp_s, rs_s, p_s = (sem(n) for n in ("max_s", "nmx_s", "exp_s", "rs_s", "p_s"))
        pt_done, pt_hi_s, pt_lo_s = sem("pt_done"), sem("pt_hi"), sem("pt_lo")
        pv_done, pv_summed = sem("pv_done"), sem("pv_summed")
        at_hi_s, at_lo_s = sem("at_hi"), sem("at_lo")
        fill_done, v_hi_s, fill_free = sem("fill_done"), sem("v_hi"), sem("fill_free")
        ld_f, deq_s, f13_hi, f13_ready, f2_hi, f2_ready = (
            sem(n) for n in ("ld_f", "deq_s", "f13_hi", "f13_ready", "f2_hi", "f2_ready"))
        ab_done, silu_s, h_s, h_hi_s, h_lo_s = (
            sem(n) for n in ("ab_done", "silu_s", "h_s", "h_hi", "h_lo"))
        o_done, o_free = sem("o_done"), sem("o_free")
        stored = sem("stored")

        def grp(stage, b):
            return 1 + HB * ORDER.index((stage, b // HB)) + b % HB

        LAST0 = grp(LN3_T, B - 1)

        def bank(g):
            return (7, 2)[(g - grp(LN3_T, HB)) % 2] if grp(LN3_T, HB) <= g <= LAST0 else g % 8

        LN4 = LAST0 + 1

        block = stack.enter_context(nc.Block())

        @block.sync
        def _(sp):
            sp.dma_start(par[:], small).then_inc(ld_small, 16)
            sp.dma_start(wqr, wq_r).then_inc(ld_small, 16)
            sp.dma_start(kyT, keysT).then_inc(ld_small, 16)
            for h in range(2):
                sp.dma_start(X[:, HB * h:HB * h + HB, :],
                             x[HB * h:HB * h + HB].rearrange("b p d -> p b d")).then_inc(ld_x[h], 16)
            sp.dma_start(rawT, ctxT.rearrange("(c p) t -> p c t", p=P)).then_inc(ld_ctxT, 16)
            sp.dma_start(rawC, ctx.rearrange("b p d -> p b d")).then_inc(ld_ctx, 16)
            sp.wait_ge(const_lo_v, DC)
            sp.dma_start(RAW1[:, :], ab).then_inc(ld_ab, 16)
            sp.wait_ge(const_lo_v, DC + 2)
            sp.wait_ge(const_lo, 2)
            sp.dma_start(mask8, mask.rearrange("b q k -> q b k")).then_inc(ld_mask, 16)
            sp.dma_start(nw, norm_w).then_inc(ld_mask, 16)
            sp.dma_start(bias_t, bias[0]).then_inc(ld_bias, 16)
            sp.wait_ge(const_lo, 2 + DC)
            for k in (WV, QK0, QK1, WO):
                sp.dma_start(RAW1[:, k * BLK:(k + 1) * BLK],
                             weights[0, :, k * BLK:(k + 1) * BLK]).then_inc(ld_w[k], 16)
            with sp.Fori(1, PAIRS) as n:
                for k in (WV, QK0, QK1, WO):
                    sp.wait_ge(const_lo, 2 + DC)
                    sp.wait_ge(w_ready[k], n)
                    sp.dma_start(RAW1[:, k * BLK:(k + 1) * BLK],
                                 weights[bass.ds(n, 1), :, k * BLK:(k + 1) * BLK]).then_inc(ld_w[k], 16)
                sp.wait_ge(mask_ready, 1)
                sp.wait_ge(bm_ready, n * 4)
                sp.dma_start(bias_t, bias[bass.ds(n, 1)]).then_inc(ld_bias, 16)

            def load_chunk(j):
                sp.dma_start(fw, words[j]).then_inc(ld_f, 16)
                sp.dma_start(fs, scales[j]).then_inc(ld_f, 16)

            for k in range(4):
                sp.wait_ge(w_ready[k], PAIRS)
            load_chunk(0)
            with sp.Fori(1, HC) as j:
                sp.wait_ge(w_ready[WO], PAIRS)
                sp.wait_ge(deq_s, j * 7)
                load_chunk(bass.ds(j, 1))
            for b in range(B):
                sp.wait_ge(o_free, 4 + B * (HC - 1) + b + 1)
                sp.dma_start(out[b], X[:, b, :]).then_inc(stored, 16)
            sp.wait_ge(stored, 16 * B)

        @block.gpsimd
        def _(pool):
            pool.memset(ident[:], 0.0).then_inc(ident_ready, 1)
            pool.memset(mhalf[:], -0.5).then_inc(ident_ready, 1)
            pool.wait_ge(ident_ready, 2)
            pool.affine_select(out=ident[:], in_=ident[:], compare_op=ALU.not_equal, fill=1.0, base=0,
                               pattern=[[-1, P]], channel_multiplier=1).then_inc(ident_ready, 1)

            def const_lows(first, chunks, hi, lo, raw):
                for c in chunks:
                    pool.wait_ge(const_hi, first + c + 1)
                    pool.tensor_tensor(lo(c), raw(c), hi(c).bitcast(F32), ALU.subtract).then_inc(const_lo, 1)

            def inverse_root(n):
                for h in range(2):
                    o = slice(HB * h, HB * h + HB)
                    pool.wait_ge(stats_ready, 2 * n - 1 + h)
                    pool.tensor_tensor(rstd[:, o], vareps[:, o], mhalf[:, o], ALU.pow).then_inc(rstd_ready, 1)

            inverse_root(1)
            const_lows(2, (2, 3), lambda c: c_hi[:, 2 * c:2 * c + 2, :], lambda c: c_lo[:, 2 * c:2 * c + 2, :],
                       lambda c: rawC[:, 2 * c:2 * c + 2, :])
            inverse_root(2)
            const_lows(2 + DC, range(DC), ab_part(0), ab_part(1), lambda c: RAW1[:, c * 1024:(c + 1) * 1024])

            def weight_lo(k, n):
                pool.wait_ge(w_hi_s[k], n + 1)
                pool.tensor_tensor(w_lo[k], RAW1[:, k * BLK:(k + 1) * BLK], w_hi[k].bitcast(F32),
                                   ALU.subtract).then_inc(w_ready[k], 1)

            weight_lo(WV, 0)
            weight_lo(QK0, 0)
            for h in range(2):
                o = slice(HB * h, HB * h + HB)
                pool.wait_ge(stats_ready, 5 + h)
                pool.tensor_tensor(rstd[:, o], vareps[:, o], mhalf[:, o], ALU.pow).then_inc(rstd_ready, 1)
                pool.wait_ge(rms_in, 1 + h)
                pool.tensor_tensor(rms[:, o], vareps[:, o], mhalf[:, o], ALU.pow).then_inc(rms_ready, 1)

            pool.wait_ge(mask_ready, 1)
            pool.wait_ge(filled, grp(LN3_T, HB - 1) + 1)
            pool.sem_inc(bm_free, 2)

            def pair(i, more):
                pool.wait_ge(ld_bias, i * 16 + 16)
                for u in range(4):
                    h, t = unit(u)
                    pool.wait_ge(bm_free, i * 4 + (u + 1))
                    pool.tensor_tensor(bm[u % 2], madd[:, HB * t:HB * t + HB, :],
                                       bias_t[:, h:h + 1, :].broadcast_to([P, HB, P]),
                                       ALU.add).then_inc(bm_ready, 1)
                    if u == 0:
                        weight_lo(QK1, i)
                weight_lo(WO, i)
                if more:
                    weight_lo(QK0, i + 1)
                    weight_lo(WV, i + 1)

            with pool.Fori(0, PAIRS - 1) as i:
                pair(i, True)
            pair(PAIRS - 1, False)

            def lows(n):
                pool.wait_ge(f13_hi, n + 1)
                pool.tensor_tensor(f_lo[:, 0:2 * DC * P], fd[:, 0:2 * DC * P],
                                   f_hi[:, 0:2 * DC * P].bitcast(F32), ALU.subtract).then_inc(f13_ready, 1)
                pool.wait_ge(f2_hi, n + 1)
                pool.tensor_tensor(f_lo[:, 2 * DC * P:CHUNK], fd[:, 2 * DC * P:CHUNK],
                                   f_hi[:, 2 * DC * P:CHUNK].bitcast(F32), ALU.subtract).then_inc(f2_ready, 1)

            inverse_root(4)
            lows(0)
            with pool.Fori(1, HC) as j:
                lows(j)

        @block.scalar
        def _(act):
            def copy(o, i, **k):
                return act.activation(o, i, ACT.Copy, **k)

            act.wait_ge(ld_small, 48)
            act.activation(gate[:], par[:], ACT.Tanh).then_inc(gates_ready, 1)

            def normalise(n, h):
                act.wait_ge(nmr_ready, 2 * n - 1 + h)
                for b in range(HB * h, HB * h + HB):
                    act.activation(XN[:, b, :], X[:, b, :], ACT.Identity, bias=nmr[:, b:b + 1],
                                   scale=rstd[:, b:b + 1]).then_inc(xn_ready, 1)

            def hi_T(g, b, dst):
                act.wait_ge(filled, g + 1)
                copy(dst[:, :, b * P:(b + 1) * P], PS[bank(g)].rearrange("p (c t) -> p c t", c=DC)
                     ).then_inc(hi0, 1)

            act.wait_ge(filled, 1)
            normalise(1, 0)
            copy(g_hi, PS[0][:, 0:DC * NE].rearrange("p (c e) -> p c e", c=DC)).then_inc(hi0, 1)
            for b in range(HB):
                hi_T(grp(LN1_T, b), b, xT_hi)
            normalise(1, 1)
            for b in range(HB, B):
                hi_T(grp(LN1_T, b), b, xT_hi)
            act.wait_ge(ld_ctxT, 16)
            for c in range(2):
                copy(cT_hi[:, c, :], rawT[:, c, :]).then_inc(const_hi, 1)

            def ctx_hi(cs):
                act.wait_ge(ld_ctx, 16)
                for c in cs:
                    copy(c_hi[:, 2 * c:2 * c + 2, :], rawC[:, 2 * c:2 * c + 2, :]).then_inc(const_hi, 1)

            for h in range(2):
                for b in half(h):
                    act.wait_ge(max0, b + 1)
                    act.activation(e0[:, b, :], s0[:, b, :], ACT.Exp, bias=negmax[:, b:b + 1],
                                   scale=float(P) ** -0.5, accum_out=esum[:, b:b + 1]).then_inc(exp0, 1)
                if h == 0:
                    ctx_hi((0, 1))
                for b in half(h):
                    act.wait_ge(rsum_ready, b + 1)
                    copy(p_hi[:, b, :], e0[:, b, :], scale=rsum[:, b:b + 1]).then_inc(p_hi0, 1)
                if h == 0:
                    ctx_hi((2, 3))
            act.wait_ge(ld_ab, 16)
            for c in range(DC):
                copy(ab_part(0)(c), RAW1[:, c * 1024:(c + 1) * 1024]).then_inc(const_hi, 1)
            for h in range(2):
                normalise(2, h)
                for b in range(HB * h, HB * h + HB):
                    hi_T(grp(LN2_T, b), b, xT_hi)
            for b in range(B):
                act.wait_ge(gate_max, b + 1)
                act.activation(eg[:, b, :], sc0[:, b, :], ACT.Exp, bias=negmax[:, b:b + 1]).then_inc(gate_exp, 1)
            for b in range(B):
                hi_T(grp(GATED_T, b), b, zT_hi)

            def weight_hi(k, n):
                act.wait_ge(ld_w[k], n * 16 + 16)
                copy(w_hi[k], RAW1[:, k * BLK:(k + 1) * BLK]).then_inc(w_hi_s[k], 1)

            weight_hi(WV, 0)
            weight_hi(QK0, 0)
            normalise(3, 0)
            for b in half(0):
                hi_T(grp(LN3_T, b), b, xT_hi)

            def pT(i, u):
                act.wait_ge(pt_done, i * 4 + u)
                copy(pT_hi, PS[2].rearrange("p (a b) -> p a b", a=HB)).then_inc(pt_hi_s, 1)

            def attended(i, u):
                h, t = unit((u - 1) % 4)
                act.wait_ge(pv_summed, i * 4 + u)
                copy(at_hi[:, h, HALF * t:HALF * t + HALF].rearrange("p (a b) -> p a b", a=HB), E
                     ).then_inc(at_hi_s, 1)

            def pair(i, first=False, last=False):
                def value(k):
                    act.wait_ge(fill_done, fills(i, k, first))
                    n = k if k < 2 else k - 4
                    copy(v_hi[:, 2 * n:2 * n + 2, :], PS[fill_bank(i, k, first)].rearrange("p (a b) -> p a b", a=2)
                         ).then_inc(v_hi_s, 1)

                if first:
                    value(V_FILLS[0][0])
                    normalise(3, 1)
                for u in range(4):
                    act.wait_ge(qk_done, i * 8 + (2 * u + 1))
                    copy(q_hi, PS[0]).then_inc(qk_hi_s, 1)
                    if u > 0 or not first:
                        pT(i, u)
                    if u == 0:
                        weight_hi(QK1, i)
                    elif u == 2:
                        weight_hi(WO, i)
                    elif u == 3 and not last:
                        weight_hi(QK0, i + 1)
                    act.wait_ge(qk_done, i * 8 + (2 * u + 2))
                    copy(k_hi, PS[1].rearrange("p (a b) -> p a b", a=HB)).then_inc(qk_hi_s, 1)
                    if u > 0 or not first:
                        attended(i, u)
                    if u in V_FILLS and not (first and u == 0):
                        value(V_FILLS[u][0])
                    act.wait_ge(nmx_s, i * 4 + (u + 1))
                    for b in range(HB):
                        exped = act.activation(E[:, b, :], S2[:, b, :], ACT.Exp, bias=u_nmx[:, b:b + 1],
                                               accum_out=u_sum[:, b:b + 1])
                    exped.then_inc(exp_s, 1)
                    if u == 3 and not last:
                        weight_hi(WV, i + 1)
                    if u in V_FILLS:
                        value(V_FILLS[u][1])
                    if first and u == 0:
                        for b in half(1):
                            hi_T(grp(LN3_T, b), b, xT_hi)

            pair(0, first=True)
            with act.Fori(1, PAIRS - 1) as i:
                pair(i)
            pair(PAIRS - 1, last=True)
            pT(PAIRS, 0)
            attended(PAIRS, 0)

            def split_13(n):
                act.wait_ge(deq_s, n * 7 + 7)
                copy(f_hi[:, 0:2 * DC * P], fd[:, 0:2 * DC * P]).then_inc(f13_hi, 1)

            def split_2(n):
                copy(f_hi[:, 2 * DC * P:CHUNK], fd[:, 2 * DC * P:CHUNK]).then_inc(f2_hi, 1)

            for h in range(2):
                normalise(4, h)
                if h == 0:
                    split_13(0)
                    split_2(0)
                for b in range(HB * h, HB * h + HB):
                    hi_T(LN4 + b, b, xT_hi)
            act.preload_act_table(ACT.Silu)

            def chunk(j, more):
                for t in range(2):
                    act.wait_ge(ab_done, j * 4 + (2 * t + 1))
                    act.activation(hbuf[t], PS[hid_bank(t, 0)], ACT.Silu).then_inc(silu_s, 1)
                    act.wait_ge(h_s, j * 2 + (t + 1))
                    copy(h_hi[:, HALF * t:HALF * t + HALF], hbuf[t]).then_inc(h_hi_s, 1)
                if more:
                    act.wait_ge(ab_done, j * 4 + 4)
                    split_13(j + 1)
                    act.wait_ge(o_done, j * 8 + 8)
                    split_2(j + 1)

            with act.Fori(0, HC - 1) as j:
                chunk(j, True)
            chunk(HC - 1, False)

        @block.vector
        def _(dve):
            own = [0]

            def step(ins):
                own[0] += 1
                return ins.then_inc(v0, 1)

            def settle():
                dve.wait_ge(v0, own[0])

            def sub(o, a, b):
                return dve.tensor_tensor(o, a, b.bitcast(F32), ALU.subtract)

            his = [0]

            def lo_T(g, b, hi, lo):
                his[0] += 1
                dve.wait_ge(hi0, his[0])
                sub(lo[:, :, b * P:(b + 1) * P], PS[bank(g)].rearrange("p (c t) -> p c t", c=DC),
                    hi[:, :, b * P:(b + 1) * P]).then_inc(drained, 1)

            def norm_stats(h):
                o = slice(HB * h, HB * h + HB)
                for b in half(h):
                    step(dve.bn_stats(stat[:, b, :], X[:, b, :]))
                settle()
                for b in half(h):
                    step(dve.bn_aggr(mv[:, b, :], stat[:, b, :]))
                settle()
                dve.tensor_scalar(vareps[:, o], mv[:, o, 1], EPS, None, ALU.add).then_inc(stats_ready, 1)

            def norm_shift(n, h):
                o = slice(HB * h, HB * h + HB)
                dve.wait_ge(rstd_ready, 2 * n - 1 + h)
                dve.scalar_tensor_tensor(nmr[:, o], mv[:, o, 0], -1.0, rstd[:, o], ALU.mult, ALU.mult
                                         ).then_inc(nmr_ready, 1)

            for h in range(2):
                dve.wait_ge(ld_x[h], 16)
                norm_stats(h)
                norm_shift(1, h)
            dve.wait_ge(hi0, 1)
            his[0] = 1
            sub(g_lo, PS[0][:, 0:DC * NE].rearrange("p (c e) -> p c e", c=DC), g_hi).then_inc(drained, 1)
            for b in range(B):
                lo_T(grp(LN1_T, b), b, xT_hi, xT_lo)
                if b == HB - 1:
                    dve.wait_ge(ld_ctxT, 16)
                    for c in (2, 3):
                        dve.tensor_copy(cT_hi[:, c, :], rawT[:, c, :]).then_inc(const_hi_v, 1)
                    for c in (2, 3):
                        dve.wait_ge(const_hi_v, c - 1)
                        sub(cT_lo[:, c, :], rawT[:, c, :], cT_hi[:, c, :]).then_inc(const_lo_v, 1)
            for c in range(2):
                dve.wait_ge(const_hi, c + 1)
                sub(cT_lo[:, c, :], rawT[:, c, :], cT_hi[:, c, :]).then_inc(const_lo_v, 1)
            scale0 = float(P) ** -0.5
            for h in range(2):
                for b in half(h):
                    dve.wait_ge(filled, grp(SIM, b) + 1)
                    step(dve.tensor_reduce(s0[:, b, :], PS[grp(SIM, b) % 8][:, 0:2 * P].rearrange(
                        "p (s k) -> p k s", s=2), AX.X, ALU.add))
                    settle()
                    step(dve.tensor_reduce(esum[:, b:b + 1], s0[:, b, :], AX.X, ALU.max))
                    settle()
                    dve.tensor_scalar(negmax[:, b:b + 1], esum[:, b:b + 1], -scale0, None, ALU.mult
                                      ).then_inc(max0, 1)
            for h in range(2):
                for b in half(h):
                    dve.wait_ge(exp0, b + 1)
                    dve.reciprocal(rsum[:, b:b + 1], esum[:, b:b + 1]).then_inc(rsum_ready, 1)
                if h == 0:
                    for c in range(2):
                        dve.wait_ge(const_hi, 2 + c + 1)
                        sub(c_lo[:, 2 * c:2 * c + 2, :], rawC[:, 2 * c:2 * c + 2, :],
                            c_hi[:, 2 * c:2 * c + 2, :]).then_inc(const_lo_v, 1)
                for b in half(h):
                    dve.wait_ge(rsum_ready, b + 1)
                    dve.wait_ge(p_hi0, b + 1)
                    dve.scalar_tensor_tensor(p_lo[:, b, :], e0[:, b, :], rsum[:, b:b + 1],
                                             p_hi[:, b, :].bitcast(F32), ALU.mult, ALU.subtract
                                             ).then_inc(drained, 1)
            dve.wait_ge(gates_ready, 1)

            def add_in(g, b, k):
                dve.wait_ge(filled, g + 1)
                dve.scalar_tensor_tensor(X[:, b, :], PS[g % 8], gate[:, k:k + 1], X[:, b, :],
                                         ALU.mult, ALU.add).then_inc(drained, 1)

            def add_half_and_norm(stage, h, k, n):
                for b in half(h):
                    add_in(grp(stage, b), b, k)
                    if h == 1 and b == HB + 1:
                        norm_shift(n, 0)
                dve.wait_ge(drained, grp(stage, HB * h + HB - 1) + 1)
                norm_stats(h)

            for h in range(2):
                add_half_and_norm(CONTEXT, h, 0, 2)
            norm_shift(2, 1)
            dve.wait_ge(const_lo, 2)
            for h in range(2):
                for b in half(h):
                    lo_T(grp(LN2_T, b), b, xT_hi, xT_lo)
                for b in half(h):
                    dve.wait_ge(filled, grp(ROUTE, b) + 1)
                    dve.tensor_reduce(sc0[:, b, :], PS[grp(ROUTE, b) % 8][:, 0:2 * NE].rearrange(
                        "p (s e) -> p e s", s=2), AX.X, ALU.add).then_inc(drained, 1)
            for h in range(2):
                o = slice(HB * h, HB * h + HB)
                dve.wait_ge(drained, grp(ROUTE, HB * h + HB - 1) + 1)
                for b in half(h):
                    step(dve.max(top[:, b, 0:8], sc0[:, b, :]))
                settle()
                for b in half(h):
                    dve.tensor_scalar(negmax[:, b:b + 1], top[:, b, 0:1], -1.0, None, ALU.mult).then_inc(gate_max, 1)
                for b in half(h):
                    step(dve.match_replace(sc1[:, b, :], top[:, b, 0:8], sc0[:, b, :], LOWEST))
                settle()
                for b in half(h):
                    step(dve.max(top[:, b, 8:16], sc1[:, b, :]))
                settle()
                for b in half(h):
                    step(dve.match_replace(sc1[:, b, :], top[:, b, 8:16], sc1[:, b, :], LOWEST))
                settle()
                dve.wait_ge(gate_exp, HB * h + HB)
                for b in half(h):
                    step(dve.scalar_tensor_tensor(eg[:, b, :], sc1[:, b, :], TAKEN, eg[:, b, :], ALU.is_le,
                                                  ALU.mult, accum_out=esum[:, b:b + 1]))
                settle()
                step(dve.reciprocal(rsum[:, o], esum[:, o]))
                settle()
                for b in half(h):
                    step(dve.tensor_scalar(eg[:, b, :], eg[:, b, :], rsum[:, b:b + 1], LORA_SCALE, ALU.mult,
                                           ALU.mult))
                settle()
                for b in half(h):
                    dve.wait_ge(filled, grp(EXPERTS, b) + 1)
                    dve.tensor_tensor(XN[:, b, :].rearrange("p (e r) -> p e r", e=NE),
                                      PS[grp(EXPERTS, b) % 8].rearrange("p (e r) -> p e r", e=NE),
                                      eg[:, b, :].rearrange("p (e o) -> p e o", o=1).broadcast_to([P, NE, RANK]),
                                      ALU.mult).then_inc(drained, 1)
            for b in range(B):
                lo_T(grp(GATED_T, b), b, zT_hi, zT_lo)

            def rms_input(h):
                o = slice(HB * h, HB * h + HB)
                settle()
                step(dve.tensor_tensor(vareps[:, o], mv[:, o, 1], rstd[:, o], ALU.mult))
                settle()
                step(dve.tensor_tensor(vareps[:, o], vareps[:, o], rstd[:, o], ALU.mult))
                settle()
                dve.tensor_scalar(vareps[:, o], vareps[:, o], EPS, None, ALU.add).then_inc(rms_in, 1)

            def attention_residual(b):
                step(dve.scalar_tensor_tensor(X[:, b, :], XN[:, b, :], gate[:, 1:2], X[:, b, :],
                                              ALU.mult, ALU.add))

            def attention_input(b):
                dve.scalar_tensor_tensor(y0[:, b, :] if b < HB else XN[:, b, :], XN[:, b, :], rms[:, b:b + 1], nw,
                                         ALU.mult, ALU.mult).then_inc(y_ready, 1)

            dve.wait_ge(ld_mask, 32)
            dve.tensor_scalar(madd, mask8, -1.0, FAR, ALU.add, ALU.mult).then_inc(mask_ready, 1)
            step(dve.tensor_reduce(keep[:], mask8, AX.X, ALU.max))
            for b in half(0):
                add_in(grp(MIX, b), b, 2)
            dve.wait_ge(drained, grp(MIX, HB - 1) + 1)
            norm_stats(0)
            add_in(grp(MIX, 4), 4, 2)
            norm_shift(3, 0)
            rms_input(0)
            add_in(grp(MIX, 5), 5, 2)
            dve.wait_ge(xn_ready, 2 * B + HB)
            dve.wait_ge(rms_ready, 1)
            attention_input(0)
            attention_input(1)
            add_in(grp(MIX, 6), 6, 2)
            attention_input(2)
            attention_input(3)
            add_in(grp(MIX, 7), 7, 2)
            dve.wait_ge(drained, grp(MIX, B - 1) + 1)
            norm_stats(1)
            for b in half(0):
                lo_T(grp(LN3_T, b), b, xT_hi, xT_lo)
            norm_shift(3, 1)
            rms_input(1)

            def dequantise(n):
                dve.wait_ge(ld_f, n * 32 + 32)
                W13 = slice(0, 2 * DC * P)
                w2 = fw[:, 2 * DC * P:CHUNK].rearrange("p (m r) -> p r m", r=4)
                for k in range(5):
                    part = fw[:, W13] if k == 0 else w2[:, k - 1, :]
                    s = CHUNK + 2 * k
                    dve.tensor_scalar(part, part, fw[:, s:s + 1], fw[:, s + 1:s + 2],
                                      ALU.logical_shift_left, ALU.arith_shift_right).then_inc(deq_s, 1)
                dve.wait_ge(deq_s, n * 7 + 5)
                dve.tensor_tensor(fd[:, W13], fw[:, W13], fs[:, W13], ALU.mult).then_inc(deq_s, 1)
                dve.tensor_tensor(fd[:, 2 * DC * P:CHUNK], fw[:, 2 * DC * P:CHUNK], fs[:, 2 * DC * P:CHUNK],
                                  ALU.mult).then_inc(deq_s, 1)

            def pT(i, u):
                dve.wait_ge(pt_hi_s, i * 4 + u)
                sub(pT_lo, PS[2].rearrange("p (a b) -> p a b", a=HB), pT_hi).then_inc(pt_lo_s, 1)

            def attended(i, u):
                h, t = unit((u - 1) % 4)
                at = slice(HALF * t, HALF * t + HALF)
                dve.wait_ge(pv_done, i * 4 + u)
                dve.tensor_reduce(E, sc.rearrange("p b (s q) -> p b q s", s=2), AX.X, ALU.add).then_inc(pv_summed, 1)
                dve.wait_ge(at_hi_s, i * 4 + u)
                sub(at_lo[:, h, at].rearrange("p (a b) -> p a b", a=HB), E,
                    at_hi[:, h, at].rearrange("p (a b) -> p a b", a=HB)).then_inc(at_lo_s, 1)


            def add_out(i, k, first=False):
                n = k + 2 if k < 6 else k - 8
                dve.wait_ge(fill_done, fills(i, k, first))
                dve.scalar_tensor_tensor(X[:, n, :], PS[fill_bank(i, k, first)], gate[:, 1:2], X[:, n, :],
                                         ALU.mult, ALU.add).then_inc(fill_free, 1)

            def pair(i, first=False, last=False):
                def value(k):
                    n = k if k < 2 else k - 4
                    dve.wait_ge(v_hi_s, i * 4 + (n + 1))
                    sub(v_lo[:, 2 * n:2 * n + 2, :], PS[fill_bank(i, k, first)].rearrange("p (a b) -> p a b", a=2),
                        v_hi[:, 2 * n:2 * n + 2, :]).then_inc(fill_free, 1)

                def maxima(u):
                    dve.wait_ge(sc_done, i * 4 + (u + 1))
                    dve.wait_ge(bm_ready, i * 4 + (u + 1))
                    dve.tensor_tensor(bm[u % 2], sc[:, :, P:2 * P], bm[u % 2], ALU.add).then_inc(bm_summed, 1)
                    dve.wait_ge(mask_ready, 1)
                    dve.wait_ge(bm_summed, i * 4 + (u + 1))
                    for b in range(HB):
                        dve.tensor_tensor_reduce(S2[:, b, :], sc[:, b, 0:P], bm[u % 2][:, b, :],
                                                 1.0, LOWEST, ALU.add, ALU.max, u_max[:, b:b + 1]
                                                 ).then_inc(max_s, 1)
                    dve.wait_ge(max_s, i * 16 + (4 * u + 4))
                    dve.tensor_scalar(u_nmx[:], u_max[:], -1.0, None, ALU.mult).then_inc(nmx_s, 1)
                    dve.sem_inc(bm_free, 1)

                def normed(u):
                    t = unit(u)[1]
                    dve.wait_ge(exp_s, i * 4 + (u + 1))
                    dve.reciprocal(u_rs[:], u_sum[:]).then_inc(rs_s, 1)
                    dve.wait_ge(rs_s, i * 8 + (2 * u + 1))
                    dve.tensor_tensor(u_rs[:], u_rs[:], keep[:, HB * t:HB * t + HB], ALU.mult).then_inc(rs_s, 1)
                    dve.wait_ge(rs_s, i * 8 + (2 * u + 2))
                    dve.tensor_tensor(E, E, u_rs[:].rearrange("p (a o) -> p a o", o=1).broadcast_to([P, HB, P]),
                                      ALU.mult).then_inc(p_s, 1)

                if first:
                    value(V_FILLS[0][0])
                    dve.wait_ge(xn_ready, 3 * B)
                    for b in half(1):
                        attention_residual(b)
                    dve.wait_ge(rms_ready, 2)
                    settle()
                for u in range(4):
                    dve.wait_ge(qk_hi_s, i * 8 + (2 * u + 1))
                    sub(q_lo, PS[0], q_hi).then_inc(qk_lo_s, 1)
                    if first and u == 0:
                        attention_input(4)
                        attention_input(5)
                    if u > 0 or not first:
                        pT(i, u)
                    dve.wait_ge(qk_hi_s, i * 8 + (2 * u + 2))
                    sub(k_lo, PS[1].rearrange("p (a b) -> p a b", a=HB), k_hi).then_inc(qk_lo_s, 1)
                    if first and u == 0:
                        attention_input(6)
                        attention_input(7)
                    if u > 0 or not first:
                        attended(i, u)
                    outs = [] if first and u == 1 else list(O_FILLS.get(u, []))
                    for k in outs[0:1]:
                        add_out(i, k, first)
                    maxima(u)
                    for k in outs[1:2]:
                        add_out(i, k, first)
                    if u in V_FILLS and not (first and u == 0):
                        value(V_FILLS[u][0])
                    normed(u)
                    for k in outs[2:4]:
                        add_out(i, k, first)
                    if u in V_FILLS:
                        value(V_FILLS[u][1])
                    if first and u == 0:
                        for b in half(1):
                            lo_T(grp(LN3_T, b), b, xT_hi, xT_lo)
                        for b in half(0):
                            attention_residual(b)
                        settle()

            pair(0, first=True)
            with dve.Fori(1, PAIRS - 1) as i:
                pair(i)
            pair(PAIRS - 1, last=True)
            pT(PAIRS, 0)
            dve.wait_ge(fill_free, 3 + 12 * PAIRS - 4)
            norm_stats(0)
            attended(PAIRS, 0)
            norm_shift(4, 0)
            dequantise(0)
            for k in O_FILLS[1]:
                add_out(PAIRS, k)

            dve.wait_ge(fill_free, 3 + 12 * PAIRS)
            norm_stats(1)
            for b in half(0):
                lo_T(LN4 + b, b, xT_hi, xT_lo)
            norm_shift(4, 1)
            for b in half(1):
                lo_T(LN4 + b, b, xT_hi, xT_lo)

            def hidden(j, t):
                dve.wait_ge(silu_s, j * 2 + (t + 1))
                dve.wait_ge(ab_done, j * 4 + (2 * t + 2))
                dve.tensor_tensor(hbuf[t], PS[hid_bank(t, 1)], hbuf[t], ALU.mult).then_inc(h_s, 1)

            def hidden_lo(j, t):
                dve.wait_ge(h_hi_s, j * 2 + (t + 1))
                at = slice(HALF * t, HALF * t + HALF)
                sub(h_lo[:, at], hbuf[t], h_hi[:, at]).then_inc(h_lo_s, 1)

            def chunk(j, more):
                if more:
                    dve.wait_ge(f13_ready, j + 1)
                    dve.wait_ge(f2_ready, j + 1)
                    dequantise(j + 1)
                hidden(j, 0)
                hidden_lo(j, 0)
                hidden(j, 1)
                hidden_lo(j, 1)
                for n in range(B):
                    dve.wait_ge(o_done, j * 8 + (n + 1))
                    dve.scalar_tensor_tensor(X[:, n, :], PS[4 + n % 4], gate[:, 3:4], X[:, n, :],
                                             ALU.mult, ALU.add).then_inc(o_free, 1)

            with dve.Fori(0, HC - 1) as j:
                chunk(j, True)
            chunk(HC - 1, False)

        @block.tensor
        def _(pe):
            def split_mm(o, wh, wl, mh, ml, first, last):
                pe.matmul(o, wh, mh, start=first, stop=False)
                pe.matmul(o, wh, ml, start=False, stop=False)
                return pe.matmul(o, wl, mh, start=False, stop=last)

            def claim(g):
                if g >= 8:
                    pe.wait_ge(drained, g - 7)
                if grp(LN3_T, HB + 2) <= g <= LAST0:
                    pe.wait_ge(drained, g - 1)
                return PS[bank(g)]

            def transpose_tile(g, b, src=XN):
                ps = claim(g)
                for c in range(DC):
                    last = pe.transpose(ps[:, c * P:(c + 1) * P], src[:, b, c * P:(c + 1) * P], ident[:])
                last.then_inc(filled, 1)

            pe.wait_ge(ld_small, 48)
            for c in range(DC):
                last = pe.matmul(PS[0][:, c * NE:(c + 1) * NE], wqr[:, c * P:(c + 1) * P], kyT,
                                 start=True, stop=True)
            last.then_inc(filled, 1)
            pe.wait_ge(ident_ready, 3)

            def product(g, ps, b, src_hi, src_lo, m_hi, m_lo):
                t = slice(b * P, (b + 1) * P)
                for c in range(DC):
                    last = split_mm(ps, src_hi[:, c, t], src_lo[:, c, t], m_hi(c), m_lo(c), c == 0, c == DC - 1)
                last.then_inc(filled, 1)

            def both_halves(g, ps, b, m):
                t = slice(b * P, (b + 1) * P)
                for c in range(DC):
                    pe.matmul(ps, xT_hi[:, c, t], m(c), start=c == 0, stop=False)
                    last = pe.matmul(ps, xT_lo[:, c, t], m(c), start=False, stop=c == DC - 1)
                last.then_inc(filled, 1)

            for stage, h in ORDER:
                if (stage, h) == (SIM, 0):
                    pe.wait_ge(const_lo_v, DC)
                if (stage, h) == (CONTEXT, 0):
                    pe.wait_ge(const_lo_v, DC + 2)
                if (stage, h) == (CONTEXT, 1):
                    pe.wait_ge(const_lo, 2)
                if (stage, h) == (EXPERTS, 0):
                    pe.wait_ge(const_lo, 2 + DC)
                for b in range(HB * h, HB * h + HB):
                    f = grp(stage, b)
                    t = slice(b * P, (b + 1) * P)
                    if stage == LN1_T:
                        pe.wait_ge(xn_ready, b + 1)
                        transpose_tile(f, b)
                    elif stage == SIM:
                        pe.wait_ge(drained, grp(LN1_T, b) + 1)
                        both_halves(f, claim(f)[:, 0:2 * P], b, lambda c: cT[:, :, c, t])
                    elif stage == CONTEXT:
                        pe.wait_ge(drained, grp(SIM, b) + 1)
                        split_mm(claim(f), p_hi[:, b, :], p_lo[:, b, :], c_hi[:, b, :], c_lo[:, b, :],
                                 True, True).then_inc(filled, 1)
                    elif stage == LN2_T:
                        pe.wait_ge(xn_ready, B + b + 1)
                        transpose_tile(f, b)
                    elif stage == ROUTE:
                        pe.wait_ge(drained, grp(LN2_T, b) + 1)
                        both_halves(f, claim(f)[:, 0:2 * NE], b, lambda c: g[:, :, c, :])
                    elif stage == EXPERTS:
                        product(f, claim(f), b, xT_hi, xT_lo, lambda c: a_hi[:, c, :], lambda c: a_lo[:, c, :])
                    elif stage == GATED_T:
                        pe.wait_ge(drained, grp(EXPERTS, b) + 1)
                        transpose_tile(f, b)
                    elif stage == MIX:
                        pe.wait_ge(drained, grp(GATED_T, b) + 1)
                        product(f, claim(f), b, zT_hi, zT_lo, lambda c: b_hi[:, c, :], lambda c: b_lo[:, c, :])
                    elif h == 0:
                        pe.wait_ge(y_ready, b + 1)
                        transpose_tile(f, b, y0)
            pe.wait_ge(drained, grp(LN3_T, HB - 1) + 1)

            pe.sem_inc(fill_free, 3)

            def transpose_p(i, u):
                pe.wait_ge(p_s, i * 4 + u)
                for b in range(HB):
                    last = pe.transpose(PS[2][:, b * P:(b + 1) * P], E[:, b, :], ident[:])
                last.then_inc(pt_done, 1)

            def attend(i, u, first=False):
                h, t = unit((u - 1) % 4)
                v = slice(h * DH, (h + 1) * DH)
                pe.wait_ge(pt_lo_s, i * 4 + u)
                if h == 0:
                    pe.wait_ge(fill_free, 3 + fills(i, V_FILLS[2 * t][1], first))
                for b in range(HB):
                    n = HB * t + b
                    pe.matmul(sc[:, b, :], v_hi[:, n, v], pp[:, b, :], start=True, stop=False)
                    last = pe.matmul(sc[:, b, :], v_lo[:, n, v], pp[:, b, :], start=False, stop=True)
                last.then_inc(pv_done, 1)

            def output_tile(i, k, h, first=False):
                n = k + 2 if k < 6 else k - 8
                if h == 0:
                    pe.wait_ge(fill_free, fills(i, k, first))
                t = slice(n * P, (n + 1) * P)
                w = slice(h * D, (h + 1) * D)
                last = split_mm(PS[fill_bank(i, k, first)], at_hi[:, h, t], at_lo[:, h, t], w_hi[WO][:, w],
                                w_lo[WO][:, w], h == 0, h == 1)
                if h == 1:
                    last.then_inc(fill_done, 1)

            def pair(i, first=False):
                def project(u, s):
                    h, half_ = unit(u)
                    hi, lo = (xT_hi, xT_lo) if s == 0 else (cT_hi, cT_lo)
                    t = slice(HALF * half_, HALF * half_ + HALF)
                    for c in range(DC):
                        w = slice((s * DC + c) * P, (s * DC + c + 1) * P)
                        last = split_mm(PS[s], w_hi[h][:, w], w_lo[h][:, w], hi[:, c, t], lo[:, c, t],
                                        c == 0, c == DC - 1)
                    last.then_inc(qk_done, 1)

                def value(k, part):
                    a, cs = part // 2, range(DC // 2 * (part % 2), DC // 2 * (part % 2 + 1))
                    n = 2 * (k if k < 2 else k - 4) + a
                    if part == 0:
                        pe.wait_ge(fill_free, fills(i, k, first))
                    t = slice(n * P, (n + 1) * P)
                    for c in cs:
                        w = slice(c * 256, (c + 1) * 256)
                        last = split_mm(PS[fill_bank(i, k, first)][:, a * 256:(a + 1) * 256], cT_hi[:, c, t],
                                        cT_lo[:, c, t], w_hi[WV][:, w], w_lo[WV][:, w], c == 0, c == DC - 1)
                    if part == 3:
                        last.then_inc(fill_done, 1)

                def scores(u):
                    pe.wait_ge(qk_lo_s, i * 8 + (2 * u + 2))
                    if u > 0 or not first:
                        pe.wait_ge(pv_summed, i * 4 + u)
                    for b in range(HB):
                        t = slice(b * P, (b + 1) * P)
                        pe.matmul(sc[:, b, :], q_hi[:, t], kk[:, b, :], start=True, stop=False)
                        last = pe.matmul(sc[:, b, :], q_lo[:, t], kk[:, b, :], start=False, stop=True)
                    last.then_inc(sc_done, 1)

                def row_fills(u, eighth):
                    if u in V_FILLS:
                        value(V_FILLS[u][eighth // 4], eighth % 4)
                    elif u == 3 or not first:
                        output_tile(i, O_FILLS[u][eighth // 2], eighth % 2, first)

                if first:
                    pe.wait_ge(w_ready[WV], i + 1)
                    for eighth in range(4):
                        row_fills(0, eighth)
                for u in range(4):
                    if u < 2:
                        pe.wait_ge(w_ready[u], i + 1)
                    project(u, 0)
                    if first and u == 1:
                        pe.wait_ge(drained, LAST0 + 1)
                    if u > 0 or not first:
                        transpose_p(i, u)
                    project(u, 1)
                    if u > 0 or not first:
                        attend(i, u, first)
                    if u == 0:
                        pe.wait_ge(w_ready[WV], i + 1)
                    if u == 1 and not first:
                        pe.wait_ge(at_lo_s, i * 4)
                    if u == 3:
                        pe.wait_ge(w_ready[WO], i + 1)
                        pe.wait_ge(at_lo_s, i * 4 + 2)
                    ahead = 4 if first and u == 0 else 0
                    for eighth in range(ahead, max(ahead, 3)):
                        row_fills(u, eighth)
                    scores(u)
                    for eighth in range(max(ahead, 3), 8):
                        row_fills(u, eighth)
                    if first and u == 0:
                        for b in half(1):
                            pe.wait_ge(y_ready, b + 1)
                            transpose_tile(grp(LN3_T, b), b)

            pair(0, first=True)
            with pe.Fori(1, PAIRS) as i:
                pair(i)
            transpose_p(PAIRS, 0)
            attend(PAIRS, 0)
            pe.wait_ge(at_lo_s, 4 * PAIRS)
            for k in O_FILLS[1]:
                output_tile(PAIRS, k, 0)
                output_tile(PAIRS, k, 1)

            pe.wait_ge(fill_free, 3 + 12 * PAIRS)
            for b in half(0):
                pe.wait_ge(xn_ready, 3 * B + b + 1)
                transpose_tile(LN4 + b, b)
            pe.wait_ge(drained, LN4 + HB)
            pe.sem_inc(o_free, 4)

            def hidden(j, t):
                at = slice(HALF * t, HALF * t + HALF)
                for m in range(2):
                    for c in range(DC):
                        w = slice((m * DC + c) * P, (m * DC + c + 1) * P)
                        last = split_mm(PS[hid_bank(t, m)], f_hi[:, w], f_lo[:, w], xT_hi[:, c, at],
                                        xT_lo[:, c, at], c == 0, c == DC - 1)
                    last.then_inc(ab_done, 1)

            def out(j):
                pe.wait_ge(f2_ready, j + 1)
                for n in range(B):
                    if n % HB == 0:
                        pe.wait_ge(h_lo_s, j * 2 + (n // HB + 1))
                    pe.wait_ge(o_free, j * 8 + (n + 1))
                    t = slice(n * P, (n + 1) * P)
                    w = slice(2 * DC * P, CHUNK)
                    split_mm(PS[4 + n % 4], h_hi[:, t], h_lo[:, t], f_hi[:, w], f_lo[:, w], True, True
                             ).then_inc(o_done, 1)

            pe.wait_ge(f13_ready, 1)
            hidden(0, 0)
            for b in half(1):
                pe.wait_ge(xn_ready, 3 * B + b + 1)
                transpose_tile(LN4 + b, b)
            pe.wait_ge(drained, LN4 + B)
            hidden(0, 1)
            out(0)
            with pe.Fori(1, HC) as j:
                pe.wait_ge(f13_ready, j + 1)
                hidden(j, 0)
                hidden(j, 1)
                out(j)


def _layouts(np, a):
    f = np.ascontiguousarray
    ctx = a["ctx_4096"]
    small = np.empty((P, 4), np.float32)
    small[:, 0:2] = a["g_xattn"]
    small[:, 2:4] = a["g_ffn"]
    by_width = lambda w: w.T.reshape(DC, P, -1).transpose(1, 0, 2)
    ab = np.concatenate([by_width(a["L0_ffn_A_w"]).reshape(P, -1), by_width(a["L0_ffn_B_w"]).reshape(P, -1)], 1)
    q, k, v = (by_width(a[f"L1_xattn_w_{n}"]).reshape(P, DC, PAIRS, 2, DH) for n in "qkv")
    weights = np.empty((PAIRS, P, 4, BLK), np.float32)
    for h in range(2):
        qk = np.stack([q[:, :, :, h], k[:, :, :, h]])
        weights[:, :, QK0 + h] = qk.transpose(3, 1, 0, 2, 4).reshape(PAIRS, P, BLK)
    weights[:, :, WV] = v.transpose(2, 0, 1, 3, 4).reshape(PAIRS, P, BLK)
    o = a["L1_xattn_w_out"].T.reshape(PAIRS, 2, DH, D)
    weights[:, :, WO] = o.transpose(0, 2, 1, 3).reshape(PAIRS, P, BLK)
    bias = a["L1_xattn_position_bias"].reshape(PAIRS, 2, P, P).transpose(0, 2, 1, 3)

    def spread(packed, s, rows, cols):
        n = np.arange(rows * cols).reshape(rows, cols)
        return packed[n // 128, n % 64].T, s[n // 64].T

    words = np.zeros((HC, P, CHUNK + SHIFTS), np.int32)
    scales = np.zeros((HC, P, CHUNK), np.float32)

    def hidden_chunks(m):
        m = np.pad(m, ((0, 0), (0, HC * P - HID)))
        return m.reshape(DC, P, HC, P).transpose(2, 1, 0, 3).reshape(HC, P, DC * P)

    for at, n in ((0, "1"), (DC * P, "3")):
        w, s = spread(a[f"L1_ffn_w{n}"], a[f"L1_ffn_s{n}"], HID, D)
        words[:, :, at:at + DC * P] = hidden_chunks(w)
        scales[:, :, at:at + DC * P] = hidden_chunks(s)
    w, s = spread(a["L1_ffn_w2"], a["L1_ffn_s2"], D, HID)
    words[:, :, 2 * DC * P:CHUNK] = np.pad(w, ((0, HC * P - HID), (0, 0))).reshape(HC, P, D)
    scales[:, :, 2 * DC * P:] = np.pad(s, ((0, HC * P - HID), (0, 0))).reshape(HC, P, D)
    low13 = (np.arange(P) // 64 % 2)[None, :, None]
    hid = np.arange(HC * P).reshape(HC, P)
    low2 = (hid[:, :, None] + HID * np.arange(4)) // 64 % 2
    low = np.concatenate([np.broadcast_to(low13, (HC, P, 1)), low2], 2)
    words[:, :, CHUNK:] = np.stack([28 * low, 4 + 24 * low], 3).reshape(HC, P, SHIFTS)
    return {
        "x": f(a["x"]), "ctx": f(ctx), "ctxT": f(ctx.reshape(T, D).T),
        "mask": f(a["mask_BxSxS2_bk0"]), "small": small,
        "norm_w": f(np.broadcast_to(a["L1_xattn_ln_weight"], (P, D))),
        "wq_r": f(a["L0_ffn_Wq_w"]), "keysT": f(a["L0_ffn_keys"].T), "ab": f(ab),
        "weights": f(weights.reshape(PAIRS, P, 4 * BLK)), "bias": f(bias),
        "words": words, "scales": scales,
    }


def kernel(**inputs):
    import numpy as np
    from concourse import bacc
    from concourse.bass_utils import run_bass_kernel_spmd

    arrays = _layouts(np, {k: np.asarray(v) for k, v in inputs.items()})
    nc = bacc.Bacc("TRN2", target_bir_lowering=False, num_devices=1)
    aps = {k: nc.dram_tensor(f"in_{k}", v.shape, mybir.dt.from_np(v.dtype), kind="ExternalInput").ap()
           for k, v in arrays.items()}
    out = nc.dram_tensor("out_x", (B, P, D), F32, kind="ExternalOutput").ap()
    gated_layers(nc, out=out, **aps)
    result = run_bass_kernel_spmd(nc, [{f"in_{k}": v for k, v in arrays.items()}], core_ids=[0])
    return result.results[0]["out_x"]
```

```python
from contextlib import ExitStack

import concourse.bass as bass
import concourse.mybir as mybir

F32 = mybir.dt.float32
F32R = mybir.dt.float32r
I32 = mybir.dt.int32
U8 = mybir.dt.uint8
ALU = mybir.AluOpType
ACT = mybir.ActivationFunctionType
AX = mybir.AxisListType

P = 128
B = 8
D = 512
DC = D // P
T = B * P
HALF = T // 2
HB = B // 2
NE, RANK, TOPK, RD = 64, 8, 16, 16
LORA_SCALE = 32 / TOPK
HEADS, DH = 32, 128
PAIRS = HEADS // 2
HID = 1376
HC = (HID + P - 1) // P
CHUNK = 2 * DC * P + D
SHIFTS = 10
EPS = 1e-5
FAR = 1e30
LOWEST = -3.0e38
TAKEN = -1.0e38

QK0, QK1, WV, WO = range(4)
BLK = 1024
(LN1_T, SIM, CONTEXT, LN2_T, ROUTE, SCORES_T, EXPERTS, GATED_T, MIX, LN3_T) = range(10)
ORDER = [(LN1_T, 0), (LN1_T, 1), (SIM, 0), (SIM, 1), (CONTEXT, 0), (CONTEXT, 1), (LN2_T, 0), (ROUTE, 0),
         (LN2_T, 1), (SCORES_T, 0), (ROUTE, 1), (EXPERTS, 0), (SCORES_T, 1), (EXPERTS, 1), (GATED_T, 0),
         (GATED_T, 1), (MIX, 0), (MIX, 1), (LN3_T, 0), (LN3_T, 1)]
WARM_START = 14
WARM = {(LN1_T, 0): 32, (LN1_T, 1): 30, (CONTEXT, 0): 10, (CONTEXT, 1): 10, (LN2_T, 0): 34, (ROUTE, 0): 20}
HALF_STAGES = (ROUTE, SCORES_T)


def gated_layers(nc, x, ctx, ctxT, mask, small, norm_w, wq_r, keysT, ab, weights, bias, words, scales, out):
    with ExitStack() as stack:
        def sb(name, shape, dt=F32):
            return stack.enter_context(nc.sbuf_tensor(name, shape, dt))

        def sem(name):
            return stack.enter_context(nc.semaphore(name))

        psum = stack.enter_context(nc.psum_tensor("psum", [P, 8, 512], F32))
        PS = [psum[:, i, :] for i in range(8)]

        X = sb("X", [P, B, D])
        XN = sb("XN", [P, B, D])
        xT_hi = sb("xT_hi", [P, DC, T], F32R)
        xT_lo = sb("xT_lo", [P, DC, T], F32R)
        cT = sb("cT", [P, 2, DC, T], F32R)
        cT_hi, cT_lo = cT[:, 0], cT[:, 1]
        RAW1 = sb("RAW1", [P, 4096])
        RAW2 = sb("RAW2", [P, 4096])
        R = sb("R", [P, 19456], F32R)

        ident = sb("ident", [P, P])
        par = sb("par", [P, 4])
        gate = sb("gate", [P, 4])
        wqr, kyT = XN[0:RD, 6, :], XN[0:RD, 7, 0:NE]
        stat = sb("stat", [P, B, 6])
        mv = sb("mv", [P, B, 2])
        vareps = sb("vareps", [P, B])
        mhalf = sb("mhalf", [P, B])
        rstd = sb("rstd", [P, B])
        nmr = sb("nmr", [P, B])
        rms = sb("rms", [P, B])
        negmax = sb("negmax", [P, B])
        esum = sb("esum", [P, B])
        rsum = sb("rsum", [P, B])
        top = sb("top", [P, B, 16])
        keep = sb("keep", [P, B])
        u_max = sb("u_max", [P, HB])
        u_nmx = sb("u_nmx", [P, HB])
        u_sum = sb("u_sum", [P, HB])
        u_rs = sb("u_rs", [P, HB])

        def cut(t, at, *dims):
            n = 1
            for d in dims:
                n *= d
            v = t[:, at:at + n]
            if len(dims) == 2:
                v = v.rearrange("p (a b) -> p a b", a=dims[0])
            if len(dims) == 3:
                v = v.rearrange("p (a b c) -> p a b c", a=dims[0], b=dims[1])
            return v

        c_hi, c_lo = cut(R, 0, B, D), cut(R, 4096, B, D)
        zT_hi, zT_lo = cut(R, 0, DC, T), cut(R, 4096, DC, T)
        a_hi, a_lo = cut(R, 8192, DC, D), cut(R, 10240, DC, D)
        b_hi, b_lo = cut(R, 12288, DC, D), cut(R, 14336, DC, D)
        p_hi, p_lo = cut(R, 16384, B, P), cut(R, 17408, B, P)
        g = cut(R, 18432, DC, 2, NE)
        g_hi, g_lo = g[:, :, 0], g[:, :, 1]
        def ab_part(half):
            def part(c):
                at = (8192, 12288)[c // 2] + 2048 * half + 1024 * (c % 2)
                return R[:, at:at + 1024]
            return part

        v_hi, v_lo = cut(R, 0, B, 256), cut(R, 2048, B, 256)
        at_hi, at_lo = cut(R, 4096, 2, T), cut(R, 6144, 2, T)
        w_hi = [R[:, 8192:9216], R[:, 12288:13312], R[:, 10240:11264], R[:, 14336:15360]]
        w_lo = [R[:, 9216:10240], R[:, 13312:14336], R[:, 11264:12288], R[:, 15360:16384]]
        q_hi, q_lo = R[:, 16384:16896], R[:, 16896:17408]
        kk = cut(R, 17408, HB, 2 * P)
        k_hi, k_lo = kk[:, :, 0:P], kk[:, :, P:2 * P]
        pp = cut(R, 18432, HB, 2 * P)
        pT_hi, pT_lo = pp[:, :, 0:P], pp[:, :, P:2 * P]
        sc = psum[:, 3:5, :].rearrange("p k (a w) -> p (k a) w", a=2)

        def unit(u):
            return u % 2, u // 2

        V_FILLS = {0: (0, 1), 2: (6, 7)}
        O_FILLS = {1: range(2, 6), 3: range(8, 12)}

        def place(i, k, first):
            if first and k < 2:
                return k
            return k - 6 if i is PAIRS else k - 4

        def fills(i, k, first):
            return i * 12 + (place(i, k, first) + 1)

        def fill_bank(i, k, first):
            return 0 if i is PAIRS and k == 5 else 5 + place(i, k, first) % 3

        def half(h):
            return range(HB * h, HB * h + HB)

        def hid_bank(t, m):
            return (2 * t + m + 1) % 4

        H_PARTS = {0: (0,), 1: (1, 2)}

        def h_cols(q):
            return slice(0, HALF) if q == 0 else slice(HALF + (q - 1) * HALF // 2, HALF + q * HALF // 2)

        def in_half(q):
            return slice(0, HALF) if q == 0 else slice((q - 1) * HALF // 2, q * HALF // 2)

        def h_part(q):
            return hbuf[min(q, 1)][:, in_half(q)]

        f_hi, f_lo = R[:, 8192:8192 + CHUNK], R[:, 8192 + CHUNK:8192 + 2 * CHUNK]
        h_hi, h_lo = R[:, 0:1024], R[:, 1024:2048]

        rawT, rawC = cut(RAW1, 0, DC, T), cut(RAW2, 0, B, D)
        madd = cut(RAW2, 0, B, P)
        bm = [cut(RAW2, 1024, HB, P), cut(RAW2, 1536, HB, P)]
        S2 = cut(RAW2, 2048, HB, P)
        E = cut(RAW2, 2560, HB, P)
        bias_t = cut(RAW2, 3072, 2, P)
        mask8 = RAW2[:, 3328:3584].bitcast(U8).rearrange("p (b k) -> p b k", b=B)
        sc0, sc1, eg = cut(RAW2, 2048, B, NE), cut(RAW2, 2560, B, NE), cut(RAW2, 1024, B, NE)
        route = RAW2[:, 1536:2048]
        e0, s0 = XN[:, :, 0:P], XN[:, :, P:2 * P]
        y0 = cut(RAW2, 1024, HB, D)
        hbuf = [RAW2[:, 2560:3072], RAW2[:, 0:512]]
        fw = RAW1[:, 0:CHUNK + SHIFTS].bitcast(I32)
        fs = RAW1[:, 2048:2048 + CHUNK]
        fd = RAW2[:, 1024:1024 + CHUNK]
        fd0 = XN[:, HB:B, :].rearrange("p b d -> p (b d)")[:, 0:CHUNK]
        nw = RAW2[:, 3584:4096]

        X_LOADS = slice(0, 2), slice(2, 4), slice(4, 8)
        ld_x = [sem(f"ld_x{n}") for n in range(3)]
        ld_small, ld_ctxT, ld_ctx, ld_ab, ld_mask, ld_bias = (
            sem(n) for n in ("ld_small", "ld_ctxT", "ld_ctx", "ld_ab", "ld_mask", "ld_bias"))
        ld_w = [sem(f"ld_w{i}") for i in range(4)]
        ident_ready = sem("ident_ready")
        const_hi, const_hi_v, const_lo_v, const_lo = (
            sem(n) for n in ("const_hi", "const_hi_v", "const_lo_v", "const_lo"))
        gates_ready = sem("gates_ready")
        stats_ready, rstd_ready, nmr_ready, xn_ready = (
            sem(n) for n in ("stats_ready", "rstd_ready", "nmr_ready", "xn_ready"))
        rms_in, rms_ready, y_ready = sem("rms_in"), sem("rms_ready"), sem("y_ready")
        filled = sem("filled")
        drained = sem("drained")
        hi0 = sem("hi0")
        max0, exp0, p_hi0 = sem("max0"), sem("exp0"), sem("p_hi0")
        gate_max, gate_exp, zg_ready = sem("gate_max"), sem("gate_exp"), sem("zg_ready")
        v0 = sem("v0")
        rsum_ready = sem("rsum_ready")
        mask_ready = sem("mask_ready")
        w_hi_s = [sem(f"w_hi{i}") for i in range(4)]
        w_ready = [sem(f"w_ready{i}") for i in range(4)]
        qk_done, qk_hi_s, qk_lo_s = sem("qk_done"), sem("qk_hi"), sem("qk_lo")
        sc_done, bm_ready, bm_free = sem("sc_done"), sem("bm_ready"), sem("bm_free")
        bm_summed = sem("bm_summed")
        max_s, nmx_s, exp_s, rs_s, p_s = (sem(n) for n in ("max_s", "nmx_s", "exp_s", "rs_s", "p_s"))
        pt_done, pt_hi_s, pt_lo_s = sem("pt_done"), sem("pt_hi"), sem("pt_lo")
        pv_done, pv_summed = sem("pv_done"), sem("pv_summed")
        at_hi_s, at_lo_s = sem("at_hi"), sem("at_lo")
        fill_done, v_hi_s, fill_free = sem("fill_done"), sem("v_hi"), sem("fill_free")
        ld_words, ld_scales, deq_s, f13_hi, f13_ready, f2_hi, f2_ready = (
            sem(n) for n in ("ld_words", "ld_scales", "deq_s", "f13_hi", "f13_ready", "f2_hi", "f2_ready"))
        ab_done, silu_s, h_s, h_hi_s, h_lo_s = (
            sem(n) for n in ("ab_done", "silu_s", "h_s", "h_hi", "h_lo"))
        o_done, o_free = sem("o_done"), sem("o_free")
        stored = sem("stored")

        def grp(stage, b):
            before = ORDER[:ORDER.index((stage, b // HB))]
            return 1 + sum(1 if st in HALF_STAGES else HB for st, _ in before) + (
                0 if stage in HALF_STAGES else b % HB)

        LAST0 = grp(LN3_T, B - 1)

        def bank(g):
            return (7, 6)[(g - grp(LN3_T, HB)) % 2] if grp(LN3_T, HB) <= g <= LAST0 else (g + 4) % 8

        LN4 = LAST0 + 1

        block = stack.enter_context(nc.Block())

        @block.sync
        def _(sp):
            for n, tiles in enumerate(X_LOADS):
                sp.dma_start(X[:, tiles, :], x[tiles].rearrange("b p d -> p b d")).then_inc(ld_x[n], 16)
                if n == 0:
                    sp.dma_start(wqr, wq_r).then_inc(ld_small, 16)
                    sp.dma_start(kyT, keysT).then_inc(ld_small, 16)
                    sp.dma_start(par[:], small).then_inc(ld_small, 16)
            sp.dma_start(rawT, ctxT.rearrange("(c p) t -> p c t", p=P)).then_inc(ld_ctxT, 16)
            sp.dma_start(rawC, ctx.rearrange("b p d -> p b d")).then_inc(ld_ctx, 16)
            sp.wait_ge(const_lo_v, DC)
            sp.dma_start(RAW1[:, :], ab).then_inc(ld_ab, 16)
            sp.wait_ge(const_lo_v, DC + 2)
            sp.wait_ge(const_lo, 2)
            sp.dma_start(mask8, mask.rearrange("b q k -> q b k")).then_inc(ld_mask, 16)
            sp.dma_start(nw, norm_w).then_inc(ld_mask, 16)
            sp.dma_start(bias_t, bias[0]).then_inc(ld_bias, 16)
            sp.wait_ge(const_lo, 2 + DC)
            for k in (WV, QK0, QK1, WO):
                sp.dma_start(RAW1[:, k * BLK:(k + 1) * BLK],
                             weights[0, :, k * BLK:(k + 1) * BLK]).then_inc(ld_w[k], 16)
            with sp.Fori(1, PAIRS) as n:
                for k in (WV, QK0, QK1, WO):
                    sp.wait_ge(const_lo, 2 + DC)
                    sp.wait_ge(w_ready[k], n)
                    sp.dma_start(RAW1[:, k * BLK:(k + 1) * BLK],
                                 weights[bass.ds(n, 1), :, k * BLK:(k + 1) * BLK]).then_inc(ld_w[k], 16)
                sp.wait_ge(mask_ready, 1)
                sp.wait_ge(bm_ready, n * 4)
                sp.dma_start(bias_t, bias[bass.ds(n, 1)]).then_inc(ld_bias, 16)

            for k in (QK0, QK1):
                sp.wait_ge(w_ready[k], PAIRS)
            sp.dma_start(fw, words[0]).then_inc(ld_words, 16)
            for k in (WV, WO):
                sp.wait_ge(w_ready[k], PAIRS)
            sp.dma_start(fs, scales[0]).then_inc(ld_scales, 16)
            with sp.Fori(1, HC) as j:
                sp.wait_ge(w_ready[WO], PAIRS)
                sp.wait_ge(deq_s, j * 7)
                sp.dma_start(fw, words[bass.ds(j, 1)]).then_inc(ld_words, 16)
                sp.dma_start(fs, scales[bass.ds(j, 1)]).then_inc(ld_scales, 16)
            for b in range(B):
                sp.wait_ge(o_free, 4 + B * (HC - 1) + b + 1)
                sp.dma_start(out[b], X[:, b, :]).then_inc(stored, 16)
            sp.wait_ge(stored, 16 * B)

        @block.gpsimd
        def _(pool):
            pool.memset(ident[:], 0.0).then_inc(ident_ready, 1)
            pool.memset(mhalf[:], -0.5).then_inc(ident_ready, 1)
            pool.wait_ge(ident_ready, 2)
            pool.affine_select(out=ident[:], in_=ident[:], compare_op=ALU.not_equal, fill=1.0, base=0,
                               pattern=[[-1, P]], channel_multiplier=1).then_inc(ident_ready, 1)

            def const_lows(first, chunks, hi, lo, raw):
                for c in chunks:
                    pool.wait_ge(const_hi, first + c + 1)
                    pool.tensor_tensor(lo(c), raw(c), hi(c).bitcast(F32), ALU.subtract).then_inc(const_lo, 1)

            def half_root(n, h):
                o = slice(HB * h, HB * h + HB)
                pool.wait_ge(stats_ready, 2 * n - 1 + h)
                pool.tensor_tensor(rstd[:, o], vareps[:, o], mhalf[:, o], ALU.pow).then_inc(rstd_ready, 1)

            def inverse_root(n):
                half_root(n, 0)
                half_root(n, 1)

            inverse_root(1)
            const_lows(2, (2, 3), lambda c: c_hi[:, 2 * c:2 * c + 2, :], lambda c: c_lo[:, 2 * c:2 * c + 2, :],
                       lambda c: rawC[:, 2 * c:2 * c + 2, :])
            def ab_lows(chunks):
                const_lows(2 + DC, chunks, ab_part(0), ab_part(1), lambda c: RAW1[:, c * 1024:(c + 1) * 1024])

            ab_lows((0, 1))
            half_root(2, 0)
            ab_lows((2, 3))
            half_root(2, 1)

            def weight_lo(k, n):
                pool.wait_ge(w_hi_s[k], n + 1)
                pool.tensor_tensor(w_lo[k], RAW1[:, k * BLK:(k + 1) * BLK], w_hi[k].bitcast(F32),
                                   ALU.subtract).then_inc(w_ready[k], 1)

            weight_lo(WV, 0)
            weight_lo(QK0, 0)
            for h in range(2):
                o = slice(HB * h, HB * h + HB)
                pool.wait_ge(stats_ready, 5 + h)
                pool.tensor_tensor(rstd[:, o], vareps[:, o], mhalf[:, o], ALU.pow).then_inc(rstd_ready, 1)
                pool.wait_ge(rms_in, 1 + h)
                pool.tensor_tensor(rms[:, o], vareps[:, o], mhalf[:, o], ALU.pow).then_inc(rms_ready, 1)

            pool.wait_ge(mask_ready, 1)
            pool.wait_ge(filled, grp(LN3_T, HB - 1) + 1)
            pool.sem_inc(bm_free, 2)

            def pair(i, more):
                pool.wait_ge(ld_bias, i * 16 + 16)
                for u in range(4):
                    h, t = unit(u)
                    pool.wait_ge(bm_free, i * 4 + (u + 1))
                    pool.tensor_tensor(bm[u % 2], madd[:, HB * t:HB * t + HB, :],
                                       bias_t[:, h:h + 1, :].broadcast_to([P, HB, P]),
                                       ALU.add).then_inc(bm_ready, 1)
                    if u == 0:
                        weight_lo(QK1, i)
                weight_lo(WO, i)
                if more:
                    weight_lo(QK0, i + 1)
                    weight_lo(WV, i + 1)

            with pool.Fori(0, PAIRS - 1) as i:
                pair(i, True)
            pair(PAIRS - 1, False)

            def lows(n, fd=fd):
                pool.wait_ge(f13_hi, n + 1)
                pool.tensor_tensor(f_lo[:, 0:2 * DC * P], fd[:, 0:2 * DC * P],
                                   f_hi[:, 0:2 * DC * P].bitcast(F32), ALU.subtract).then_inc(f13_ready, 1)
                pool.wait_ge(f2_hi, n + 1)
                pool.tensor_tensor(f_lo[:, 2 * DC * P:CHUNK], fd[:, 2 * DC * P:CHUNK],
                                   f_hi[:, 2 * DC * P:CHUNK].bitcast(F32), ALU.subtract).then_inc(f2_ready, 1)

            lows(0, fd0)
            inverse_root(4)
            with pool.Fori(1, HC) as j:
                lows(j)

        @block.scalar
        def _(act):
            def copy(o, i, **k):
                return act.activation(o, i, ACT.Copy, **k)

            act.wait_ge(ld_small, 48)
            act.activation(gate[:], par[:], ACT.Tanh).then_inc(gates_ready, 1)

            def normalise(n, h):
                act.wait_ge(nmr_ready, 2 * n - 1 + h)
                for b in range(HB * h, HB * h + HB):
                    act.activation(XN[:, b, :], X[:, b, :], ACT.Identity, bias=nmr[:, b:b + 1],
                                   scale=rstd[:, b:b + 1]).then_inc(xn_ready, 1)

            def hi_T(g, b, dst):
                act.wait_ge(filled, g + 1)
                copy(dst[:, :, b * P:(b + 1) * P], PS[bank(g)].rearrange("p (c t) -> p c t", c=DC)
                     ).then_inc(hi0, 1)

            normalise(1, 0)
            act.wait_ge(filled, 1)
            copy(g_hi, PS[bank(0)][:, 0:DC * NE].rearrange("p (c e) -> p c e", c=DC)).then_inc(hi0, 1)
            for b in range(HB):
                hi_T(grp(LN1_T, b), b, xT_hi)
            act.wait_ge(ld_ctxT, 16)
            for c in range(2):
                copy(cT_hi[:, c, :], rawT[:, c, :]).then_inc(const_hi, 1)
            normalise(1, 1)
            for b in range(HB, B):
                hi_T(grp(LN1_T, b), b, xT_hi)

            act.wait_ge(ld_ctx, 16)
            for c in range(DC):
                copy(c_hi[:, 2 * c:2 * c + 2, :], rawC[:, 2 * c:2 * c + 2, :]).then_inc(const_hi, 1)

            for h in range(2):
                for b in half(h):
                    act.wait_ge(max0, b + 1)
                    act.activation(e0[:, b, :], s0[:, b, :], ACT.Exp, bias=negmax[:, b:b + 1],
                                   scale=float(P) ** -0.5, accum_out=esum[:, b:b + 1]).then_inc(exp0, 1)
                for b in half(h):
                    act.wait_ge(rsum_ready, b + 1)
                    copy(p_hi[:, b, :], e0[:, b, :], scale=rsum[:, b:b + 1]).then_inc(p_hi0, 1)
            act.wait_ge(ld_ab, 16)
            for c in range(DC):
                copy(ab_part(0)(c), RAW1[:, c * 1024:(c + 1) * 1024]).then_inc(const_hi, 1)
            for h in range(2):
                normalise(2, h)
                for b in range(HB * h, HB * h + HB):
                    hi_T(grp(LN2_T, b), b, xT_hi)
            for b in range(B):
                act.wait_ge(gate_max, b + 1)
                act.activation(eg[:, b, :], sc0[:, b, :], ACT.Exp, bias=negmax[:, b:b + 1]).then_inc(gate_exp, 1)
            for b in range(B):
                hi_T(grp(GATED_T, b), b, zT_hi)

            def weight_hi(k, n):
                act.wait_ge(ld_w[k], n * 16 + 16)
                copy(w_hi[k], RAW1[:, k * BLK:(k + 1) * BLK]).then_inc(w_hi_s[k], 1)

            weight_hi(WV, 0)
            weight_hi(QK0, 0)
            normalise(3, 0)
            for b in half(0):
                hi_T(grp(LN3_T, b), b, xT_hi)

            def split_13(n, fd=fd):
                act.wait_ge(deq_s, n * 7 + 6)
                copy(f_hi[:, 0:2 * DC * P], fd[:, 0:2 * DC * P]).then_inc(f13_hi, 1)

            def split_2(n, fd=fd):
                act.wait_ge(deq_s, n * 7 + 7)
                copy(f_hi[:, 2 * DC * P:CHUNK], fd[:, 2 * DC * P:CHUNK]).then_inc(f2_hi, 1)

            def pT(i, u):
                act.wait_ge(pt_done, i * 4 + u)
                copy(pT_hi, PS[2].rearrange("p (a b) -> p a b", a=HB)).then_inc(pt_hi_s, 1)

            def attended(i, u):
                h, t = unit((u - 1) % 4)
                act.wait_ge(pv_summed, i * 4 + u)
                copy(at_hi[:, h, HALF * t:HALF * t + HALF].rearrange("p (a b) -> p a b", a=HB), E
                     ).then_inc(at_hi_s, 1)

            def pair(i, first=False, last=False):
                def value(k):
                    act.wait_ge(fill_done, fills(i, k, first))
                    n = k if k < 2 else k - 4
                    copy(v_hi[:, 2 * n:2 * n + 2, :], PS[fill_bank(i, k, first)].rearrange("p (a b) -> p a b", a=2)
                         ).then_inc(v_hi_s, 1)

                if first:
                    value(V_FILLS[0][0])
                for u in range(4):
                    act.wait_ge(qk_done, i * 8 + (2 * u + 1))
                    copy(q_hi, PS[0]).then_inc(qk_hi_s, 1)
                    if u > 0 or not first:
                        pT(i, u)
                    if u == 0:
                        weight_hi(QK1, i)
                    elif u == 2:
                        weight_hi(WO, i)
                    elif u == 3 and not last:
                        weight_hi(QK0, i + 1)
                    act.wait_ge(qk_done, i * 8 + (2 * u + 2))
                    copy(k_hi, PS[1].rearrange("p (a b) -> p a b", a=HB)).then_inc(qk_hi_s, 1)
                    if first and u == 0:
                        normalise(3, 1)
                    if first and u == 1:
                        hi_T(grp(LN3_T, 4), 4, xT_hi)
                        hi_T(grp(LN3_T, 5), 5, xT_hi)
                    if u > 0 or not first:
                        attended(i, u)
                    if first and u == 1:
                        hi_T(grp(LN3_T, 6), 6, xT_hi)
                        hi_T(grp(LN3_T, 7), 7, xT_hi)
                    if u in V_FILLS and not (first and u == 0):
                        value(V_FILLS[u][0])
                    if u == 3 and last:
                        split_13(0, fd0)
                    act.wait_ge(nmx_s, i * 4 + (u + 1))
                    for b in range(HB):
                        exped = act.activation(E[:, b, :], S2[:, b, :], ACT.Exp, bias=u_nmx[:, b:b + 1],
                                               accum_out=u_sum[:, b:b + 1])
                    exped.then_inc(exp_s, 1)
                    if u == 3 and last:
                        split_2(0, fd0)
                    elif u == 3:
                        weight_hi(WV, i + 1)
                    if u in V_FILLS:
                        value(V_FILLS[u][1])

            pair(0, first=True)
            with act.Fori(1, PAIRS - 1) as i:
                pair(i)
            pair(PAIRS - 1, last=True)
            pT(PAIRS, 0)
            attended(PAIRS, 0)

            normalise(4, 0)
            for b in half(0):
                hi_T(LN4 + b, b, xT_hi)
            normalise(4, 1)
            for b in half(1):
                hi_T(LN4 + b, b, xT_hi)
            act.preload_act_table(ACT.Silu)

            def chunk(j, more):
                for t in range(2):
                    act.wait_ge(ab_done, j * 4 + (2 * t + 1))
                    act.activation(hbuf[t], PS[hid_bank(t, 0)], ACT.Silu).then_inc(silu_s, 1)
                    for q in H_PARTS[t]:
                        act.wait_ge(h_s, j * 3 + (q + 1))
                        copy(h_hi[:, h_cols(q)], h_part(q)).then_inc(h_hi_s, 1)
                if more:
                    act.wait_ge(ab_done, j * 4 + 4)
                    split_13(j + 1)
                    act.wait_ge(o_done, j * 8 + 8)
                    split_2(j + 1)

            with act.Fori(0, HC - 1) as j:
                chunk(j, True)
            chunk(HC - 1, False)

        @block.vector
        def _(dve):
            own = [0]

            def step(ins):
                own[0] += 1
                return ins.then_inc(v0, 1)

            def settle():
                dve.wait_ge(v0, own[0])

            def sub(o, a, b):
                return dve.tensor_tensor(o, a, b.bitcast(F32), ALU.subtract)

            his = [0]

            def lo_T(g, b, hi, lo):
                his[0] += 1
                dve.wait_ge(hi0, his[0])
                sub(lo[:, :, b * P:(b + 1) * P], PS[bank(g)].rearrange("p (c t) -> p c t", c=DC),
                    hi[:, :, b * P:(b + 1) * P]).then_inc(drained, 1)

            def tile_stats(b):
                step(dve.bn_stats(stat[:, b, :], X[:, b, :]))

            def half_stats(h):
                o = slice(HB * h, HB * h + HB)
                settle()
                for b in half(h):
                    step(dve.bn_aggr(mv[:, b, :], stat[:, b, :]))
                settle()
                dve.tensor_scalar(vareps[:, o], mv[:, o, 1], EPS, None, ALU.add).then_inc(stats_ready, 1)

            def norm_shift(n, h):
                o = slice(HB * h, HB * h + HB)
                dve.wait_ge(rstd_ready, 2 * n - 1 + h)
                dve.scalar_tensor_tensor(nmr[:, o], mv[:, o, 0], -1.0, rstd[:, o], ALU.mult, ALU.mult
                                         ).then_inc(nmr_ready, 1)

            for h in range(2):
                for b in half(h):
                    if b in (0, 2, 4):
                        dve.wait_ge(ld_x[b // 2], 16)
                    tile_stats(b)
                half_stats(h)
                norm_shift(1, h)
            dve.wait_ge(hi0, 1)
            his[0] = 1
            sub(g_lo, PS[bank(0)][:, 0:DC * NE].rearrange("p (c e) -> p c e", c=DC), g_hi).then_inc(drained, 1)
            for b in half(0):
                lo_T(grp(LN1_T, b), b, xT_hi, xT_lo)
            dve.wait_ge(ld_ctxT, 16)
            for c in (2, 3):
                dve.tensor_copy(cT_hi[:, c, :], rawT[:, c, :]).then_inc(const_hi_v, 1)
            for c in (2, 3, 0, 1):
                if c >= 2:
                    dve.wait_ge(const_hi_v, c - 1)
                else:
                    dve.wait_ge(const_hi, c + 1)
                sub(cT_lo[:, c, :], rawT[:, c, :], cT_hi[:, c, :]).then_inc(const_lo_v, 1)
            for b in half(1):
                lo_T(grp(LN1_T, b), b, xT_hi, xT_lo)
            scale0 = float(P) ** -0.5
            for h in range(2):
                for b in half(h):
                    dve.wait_ge(filled, grp(SIM, b) + 1)
                    step(dve.tensor_reduce(s0[:, b, :], PS[bank(grp(SIM, b))][:, 0:2 * P].rearrange(
                        "p (s k) -> p k s", s=2), AX.X, ALU.add))
                    settle()
                    step(dve.tensor_reduce(esum[:, b:b + 1], s0[:, b, :], AX.X, ALU.max))
                    settle()
                    dve.tensor_scalar(negmax[:, b:b + 1], esum[:, b:b + 1], -scale0, None, ALU.mult
                                      ).then_inc(max0, 1)
                if h == 0:
                    for c in range(2):
                        dve.wait_ge(const_hi, 2 + c + 1)
                        sub(c_lo[:, 2 * c:2 * c + 2, :], rawC[:, 2 * c:2 * c + 2, :],
                            c_hi[:, 2 * c:2 * c + 2, :]).then_inc(const_lo_v, 1)
                for b in half(h):
                    dve.wait_ge(exp0, b + 1)
                    dve.reciprocal(rsum[:, b:b + 1], esum[:, b:b + 1]).then_inc(rsum_ready, 1)
                for b in half(h):
                    dve.wait_ge(rsum_ready, b + 1)
                    dve.wait_ge(p_hi0, b + 1)
                    dve.scalar_tensor_tensor(p_lo[:, b, :], e0[:, b, :], rsum[:, b:b + 1],
                                             p_hi[:, b, :].bitcast(F32), ALU.mult, ALU.subtract
                                             ).then_inc(drained, 1)
            dve.wait_ge(gates_ready, 1)

            def add_in(g, b, k):
                dve.wait_ge(filled, g + 1)
                dve.scalar_tensor_tensor(X[:, b, :], PS[bank(g)], gate[:, k:k + 1], X[:, b, :],
                                         ALU.mult, ALU.add).then_inc(drained, 1)

            def tile_stats_of(stage, b):
                dve.wait_ge(drained, grp(stage, b) + 1)
                tile_stats(b)

            def add_half_and_norm(stage, h, k, n):
                for b in half(h):
                    add_in(grp(stage, b), b, k)
                    if h == 1 and b == HB + 1:
                        norm_shift(n, 0)
                    if b > HB * h:
                        tile_stats_of(stage, b - 1)
                tile_stats_of(stage, HB * h + HB - 1)
                half_stats(h)

            for h in range(2):
                add_half_and_norm(CONTEXT, h, 0, 2)

            def route_out(h):
                dve.wait_ge(filled, grp(ROUTE, HB * h) + 1)
                dve.tensor_copy(route, PS[bank(grp(ROUTE, HB * h))]).then_inc(drained, 1)

            def scores_out(h):
                f = grp(SCORES_T, HB * h)
                dve.wait_ge(filled, f + 1)
                dve.tensor_reduce(sc0[:, HB * h:HB * h + HB, :], PS[bank(f)].rearrange(
                    "p (b s e) -> p b e s", b=HB, s=2), AX.X, ALU.add).then_inc(drained, 1)

            def gate_half(h):
                o = slice(HB * h, HB * h + HB)
                dve.wait_ge(drained, grp(SCORES_T, HB * h) + 1)
                for b in half(h):
                    step(dve.max(top[:, b, 0:8], sc0[:, b, :]))
                settle()
                for b in half(h):
                    dve.tensor_scalar(negmax[:, b:b + 1], top[:, b, 0:1], -1.0, None, ALU.mult).then_inc(gate_max, 1)
                for b in half(h):
                    step(dve.match_replace(sc1[:, b, :], top[:, b, 0:8], sc0[:, b, :], LOWEST))
                settle()
                for b in half(h):
                    step(dve.max(top[:, b, 8:16], sc1[:, b, :]))
                settle()
                for b in half(h):
                    step(dve.match_replace(sc1[:, b, :], top[:, b, 8:16], sc1[:, b, :], LOWEST))
                settle()
                dve.wait_ge(gate_exp, HB * h + HB)
                for b in half(h):
                    step(dve.scalar_tensor_tensor(eg[:, b, :], sc1[:, b, :], TAKEN, eg[:, b, :], ALU.is_le,
                                                  ALU.mult, accum_out=esum[:, b:b + 1]))
                settle()
                step(dve.reciprocal(rsum[:, o], esum[:, o]))
                settle()
                for b in half(h):
                    step(dve.tensor_scalar(eg[:, b, :], eg[:, b, :], rsum[:, b:b + 1], LORA_SCALE, ALU.mult,
                                           ALU.mult))
                settle()

            def gate_experts(h):
                for b in half(h):
                    dve.wait_ge(filled, grp(EXPERTS, b) + 1)
                    dve.tensor_tensor(XN[:, b, :].rearrange("p (e r) -> p e r", e=NE),
                                      PS[bank(grp(EXPERTS, b))].rearrange("p (e r) -> p e r", e=NE),
                                      eg[:, b, :].rearrange("p (e o) -> p e o", o=1).broadcast_to([P, NE, RANK]),
                                      ALU.mult).then_inc(drained, 1)

            for b in half(0):
                lo_T(grp(LN2_T, b), b, xT_hi, xT_lo)
                if b == 1:
                    norm_shift(2, 1)
            dve.wait_ge(const_lo, 2)
            route_out(0)
            for b in half(1):
                lo_T(grp(LN2_T, b), b, xT_hi, xT_lo)
            scores_out(0)
            route_out(1)
            gate_half(0)
            gate_experts(0)
            scores_out(1)
            gate_half(1)
            gate_experts(1)
            for b in range(B):
                lo_T(grp(GATED_T, b), b, zT_hi, zT_lo)

            def rms_input(h):
                o = slice(HB * h, HB * h + HB)
                settle()
                step(dve.tensor_tensor(vareps[:, o], mv[:, o, 1], rstd[:, o], ALU.mult))
                settle()
                step(dve.tensor_tensor(vareps[:, o], vareps[:, o], rstd[:, o], ALU.mult))
                settle()
                dve.tensor_scalar(vareps[:, o], vareps[:, o], EPS, None, ALU.add).then_inc(rms_in, 1)

            def attention_residual(b):
                step(dve.scalar_tensor_tensor(X[:, b, :], XN[:, b, :], gate[:, 1:2], X[:, b, :],
                                              ALU.mult, ALU.add))

            def attention_input(b):
                dve.scalar_tensor_tensor(y0[:, b, :] if b < HB else XN[:, b, :], XN[:, b, :], rms[:, b:b + 1], nw,
                                         ALU.mult, ALU.mult).then_inc(y_ready, 1)

            dve.wait_ge(ld_mask, 32)
            dve.tensor_scalar(madd, mask8, -1.0, FAR, ALU.add, ALU.mult).then_inc(mask_ready, 1)
            step(dve.tensor_reduce(keep[:], mask8, AX.X, ALU.max))
            for b in half(0):
                add_in(grp(MIX, b), b, 2)
                if b > 0:
                    tile_stats_of(MIX, b - 1)
            tile_stats_of(MIX, HB - 1)
            half_stats(0)
            add_in(grp(MIX, 4), 4, 2)
            norm_shift(3, 0)
            rms_input(0)
            add_in(grp(MIX, 5), 5, 2)
            dve.wait_ge(xn_ready, 2 * B + HB)
            dve.wait_ge(rms_ready, 1)
            attention_input(0)
            attention_input(1)
            add_in(grp(MIX, 6), 6, 2)
            attention_input(2)
            attention_input(3)
            add_in(grp(MIX, 7), 7, 2)
            for b in half(0):
                lo_T(grp(LN3_T, b), b, xT_hi, xT_lo)
            for b in half(1):
                tile_stats_of(MIX, b)
            half_stats(1)

            def nibbles(n):
                dve.wait_ge(ld_words, n * 16 + 16)
                w2 = fw[:, 2 * DC * P:CHUNK].rearrange("p (m r) -> p r m", r=4)
                for k in range(5):
                    part = fw[:, 0:2 * DC * P] if k == 0 else w2[:, k - 1, :]
                    s = CHUNK + 2 * k
                    dve.tensor_scalar(part, part, fw[:, s:s + 1], fw[:, s + 1:s + 2],
                                      ALU.logical_shift_left, ALU.arith_shift_right).then_inc(deq_s, 1)

            W_PARTS = slice(0, 2 * DC * P), slice(2 * DC * P, CHUNK)

            def scaled(n, part, fd=fd):
                dve.wait_ge(ld_scales, n * 16 + 16)
                dve.wait_ge(deq_s, n * 7 + 5)
                dve.tensor_tensor(fd[:, part], fw[:, part], fs[:, part], ALU.mult).then_inc(deq_s, 1)

            def dequantise(n):
                nibbles(n)
                for part in W_PARTS:
                    scaled(n, part)

            def pT(i, u):
                dve.wait_ge(pt_hi_s, i * 4 + u)
                sub(pT_lo, PS[2].rearrange("p (a b) -> p a b", a=HB), pT_hi).then_inc(pt_lo_s, 1)

            def attended(i, u):
                h, t = unit((u - 1) % 4)
                at = slice(HALF * t, HALF * t + HALF)
                dve.wait_ge(pv_done, i * 4 + u)
                dve.tensor_reduce(E, sc.rearrange("p b (s q) -> p b q s", s=2), AX.X, ALU.add).then_inc(pv_summed, 1)
                dve.wait_ge(at_hi_s, i * 4 + u)
                sub(at_lo[:, h, at].rearrange("p (a b) -> p a b", a=HB), E,
                    at_hi[:, h, at].rearrange("p (a b) -> p a b", a=HB)).then_inc(at_lo_s, 1)


            def add_out(i, k, first=False):
                n = k + 2 if k < 6 else k - 8
                dve.wait_ge(fill_done, fills(i, k, first))
                dve.scalar_tensor_tensor(X[:, n, :], PS[fill_bank(i, k, first)], gate[:, 1:2], X[:, n, :],
                                         ALU.mult, ALU.add).then_inc(fill_free, 1)

            def added_stats(k, i=PAIRS - 1):
                dve.wait_ge(fill_free, 3 + fills(i, k, False))
                tile_stats(k + 2 if k < 6 else k - 8)

            def pair(i, first=False, last=False):
                def value(k):
                    n = k if k < 2 else k - 4
                    dve.wait_ge(v_hi_s, i * 4 + (n + 1))
                    sub(v_lo[:, 2 * n:2 * n + 2, :], PS[fill_bank(i, k, first)].rearrange("p (a b) -> p a b", a=2),
                        v_hi[:, 2 * n:2 * n + 2, :]).then_inc(fill_free, 1)

                def maxima(u):
                    dve.wait_ge(sc_done, i * 4 + (u + 1))
                    dve.wait_ge(bm_ready, i * 4 + (u + 1))
                    dve.tensor_tensor(bm[u % 2], sc[:, :, P:2 * P], bm[u % 2], ALU.add).then_inc(bm_summed, 1)
                    dve.wait_ge(mask_ready, 1)
                    dve.wait_ge(bm_summed, i * 4 + (u + 1))
                    for b in range(HB):
                        dve.tensor_tensor_reduce(S2[:, b, :], sc[:, b, 0:P], bm[u % 2][:, b, :],
                                                 1.0, LOWEST, ALU.add, ALU.max, u_max[:, b:b + 1]
                                                 ).then_inc(max_s, 1)
                    dve.wait_ge(max_s, i * 16 + (4 * u + 4))
                    dve.tensor_scalar(u_nmx[:], u_max[:], -1.0, None, ALU.mult).then_inc(nmx_s, 1)
                    dve.sem_inc(bm_free, 1)

                def normed(u):
                    t = unit(u)[1]
                    dve.wait_ge(exp_s, i * 4 + (u + 1))
                    dve.reciprocal(u_rs[:], u_sum[:]).then_inc(rs_s, 1)
                    dve.wait_ge(rs_s, i * 8 + (2 * u + 1))
                    dve.tensor_tensor(u_rs[:], u_rs[:], keep[:, HB * t:HB * t + HB], ALU.mult).then_inc(rs_s, 1)
                    dve.wait_ge(rs_s, i * 8 + (2 * u + 2))
                    dve.tensor_tensor(E, E, u_rs[:].rearrange("p (a o) -> p a o", o=1).broadcast_to([P, HB, P]),
                                      ALU.mult).then_inc(p_s, 1)

                if first:
                    value(V_FILLS[0][0])
                for u in range(4):
                    dve.wait_ge(qk_hi_s, i * 8 + (2 * u + 1))
                    sub(q_lo, PS[0], q_hi).then_inc(qk_lo_s, 1)
                    if first and u == 0:
                        norm_shift(3, 1)
                        rms_input(1)
                    if u > 0 or not first:
                        pT(i, u)
                    if u == 2 and last:
                        nibbles(0)
                    if u == 3 and last:
                        scaled(0, W_PARTS[0], fd0)
                    dve.wait_ge(qk_hi_s, i * 8 + (2 * u + 2))
                    sub(k_lo, PS[1].rearrange("p (a b) -> p a b", a=HB), k_hi).then_inc(qk_lo_s, 1)
                    if first and u == 1:
                        for b in (4, 5):
                            lo_T(grp(LN3_T, b), b, xT_hi, xT_lo)
                    if u > 0 or not first:
                        attended(i, u)
                    if first and u == 1:
                        for b in (6, 7):
                            lo_T(grp(LN3_T, b), b, xT_hi, xT_lo)
                    outs = [] if first and u == 1 else list(O_FILLS.get(u, []))
                    for k in outs[0:1]:
                        add_out(i, k, first)
                    maxima(u)
                    if first and u == 0:
                        dve.wait_ge(xn_ready, 3 * B)
                        attention_residual(4)
                        attention_residual(5)
                    for k in outs[1:2]:
                        add_out(i, k, first)
                    if u == 3 and last:
                        scaled(0, W_PARTS[1], fd0)
                    if u in V_FILLS and not (first and u == 0):
                        value(V_FILLS[u][0])
                    normed(u)
                    for k in outs[2:4]:
                        add_out(i, k, first)
                    if u in V_FILLS:
                        value(V_FILLS[u][1])
                    if first and u == 0:
                        attention_residual(6)
                        attention_residual(7)
                        settle()
                        dve.wait_ge(rms_ready, 2)
                        for b in half(1):
                            attention_input(b)
                    if first and u == 1:
                        for b in half(0):
                            attention_residual(b)
                        settle()

            pair(0, first=True)
            with dve.Fori(1, PAIRS - 1) as i:
                pair(i)
            pair(PAIRS - 1, last=True)
            added_stats(8)
            added_stats(9)
            pT(PAIRS, 0)
            added_stats(10)
            added_stats(11)
            half_stats(0)
            attended(PAIRS, 0)
            norm_shift(4, 0)
            for k in (2, 3):
                add_out(PAIRS, k)
                added_stats(k, PAIRS)
            for b in half(0):
                lo_T(LN4 + b, b, xT_hi, xT_lo)
            for k in (4, 5):
                add_out(PAIRS, k)
                added_stats(k, PAIRS)

            half_stats(1)
            norm_shift(4, 1)
            for b in half(1):
                lo_T(LN4 + b, b, xT_hi, xT_lo)

            def hidden(j, t):
                dve.wait_ge(silu_s, j * 2 + (t + 1))
                dve.wait_ge(ab_done, j * 4 + (2 * t + 2))
                for q in H_PARTS[t]:
                    dve.tensor_tensor(h_part(q), PS[hid_bank(t, 1)][:, in_half(q)], h_part(q), ALU.mult
                                      ).then_inc(h_s, 1)

            def hidden_lo(j, t):
                for q in H_PARTS[t]:
                    dve.wait_ge(h_hi_s, j * 3 + (q + 1))
                    sub(h_lo[:, h_cols(q)], h_part(q), h_hi[:, h_cols(q)]).then_inc(h_lo_s, 1)

            def chunk(j, more):
                if more:
                    dve.wait_ge(f13_ready, j + 1)
                    dve.wait_ge(f2_ready, j + 1)
                    dequantise(j + 1)
                hidden(j, 0)
                hidden_lo(j, 0)
                hidden(j, 1)
                hidden_lo(j, 1)
                for n in range(B):
                    dve.wait_ge(o_done, j * 8 + (n + 1))
                    dve.scalar_tensor_tensor(X[:, n, :], PS[4 + n % 4], gate[:, 3:4], X[:, n, :],
                                             ALU.mult, ALU.add).then_inc(o_free, 1)

            with dve.Fori(0, HC - 1) as j:
                chunk(j, True)
            chunk(HC - 1, False)

        @block.tensor
        def _(pe):
            def split_mm(o, wh, wl, mh, ml, first, last):
                pe.matmul(o, wh, mh, start=first, stop=False)
                pe.matmul(o, wh, ml, start=False, stop=False)
                return pe.matmul(o, wl, mh, start=False, stop=last)

            def claim(g):
                if g >= 8:
                    pe.wait_ge(drained, g - 7)
                if grp(LN3_T, HB + 2) <= g <= LAST0:
                    pe.wait_ge(drained, g - 1)
                return PS[bank(g)]

            def transpose_tile(g, b, src=XN):
                ps = claim(g)
                for c in range(DC):
                    last = pe.transpose(ps[:, c * P:(c + 1) * P], src[:, b, c * P:(c + 1) * P], ident[:])
                last.then_inc(filled, 1)

            def keep_warm(ps, n):
                for _ in range(n):
                    pe.transpose(ps[:, 0:P], ident[:], ident[:])

            pe.wait_ge(ident_ready, 3)
            keep_warm(PS[bank(0)], WARM_START)
            pe.wait_ge(ld_small, 48)
            for c in range(DC):
                last = pe.matmul(PS[bank(0)][:, c * NE:(c + 1) * NE], wqr[:, c * P:(c + 1) * P], kyT,
                                 start=True, stop=True)
            last.then_inc(filled, 1)

            def product(g, ps, b, src_hi, src_lo, m_hi, m_lo):
                t = slice(b * P, (b + 1) * P)
                for c in range(DC):
                    last = split_mm(ps, src_hi[:, c, t], src_lo[:, c, t], m_hi(c), m_lo(c), c == 0, c == DC - 1)
                last.then_inc(filled, 1)

            def both_halves(g, ps, b, m):
                t = slice(b * P, (b + 1) * P)
                for c in range(DC):
                    pe.matmul(ps, xT_hi[:, c, t], m(c), start=c == 0, stop=False)
                    last = pe.matmul(ps, xT_lo[:, c, t], m(c), start=False, stop=c == DC - 1)
                last.then_inc(filled, 1)

            for stage, h in ORDER:
                keep_warm(claim(grp(stage, HB * h)), WARM.get((stage, h), 0))
                if (stage, h) == (SIM, 0):
                    pe.wait_ge(const_lo_v, DC)
                if (stage, h) == (CONTEXT, 0):
                    pe.wait_ge(const_lo_v, DC + 2)
                if (stage, h) == (CONTEXT, 1):
                    pe.wait_ge(const_lo, 2)
                if (stage, h) == (EXPERTS, 0):
                    pe.wait_ge(const_lo, 2 + 2)
                if (stage, h) == (MIX, 0):
                    pe.wait_ge(const_lo, 2 + DC)
                if stage == ROUTE:
                    f, t = grp(stage, HB * h), slice(HALF * h, HALF * h + HALF)
                    ps = claim(f)
                    pe.wait_ge(drained, grp(LN2_T, HB * h + HB - 1) + 1)
                    for c in range(DC):
                        pe.matmul(ps, g[:, c].rearrange("p s e -> p (s e)"), xT_hi[:, c, t], start=c == 0,
                                  stop=False)
                        last = pe.matmul(ps, g[:, c].rearrange("p s e -> p (s e)"), xT_lo[:, c, t], start=False,
                                         stop=c == DC - 1)
                    last.then_inc(filled, 1)
                    continue
                if stage == SCORES_T:
                    f = grp(stage, HB * h)
                    ps = claim(f)
                    pe.wait_ge(drained, grp(ROUTE, HB * h) + 1)
                    for b in range(HB):
                        last = pe.transpose(ps[:, b * P:(b + 1) * P], route[:, b * P:(b + 1) * P], ident[:])
                    last.then_inc(filled, 1)
                    continue
                for b in range(HB * h, HB * h + HB):
                    f = grp(stage, b)
                    t = slice(b * P, (b + 1) * P)
                    if stage == LN1_T:
                        pe.wait_ge(xn_ready, b + 1)
                        transpose_tile(f, b)
                    elif stage == SIM:
                        pe.wait_ge(drained, grp(LN1_T, b) + 1)
                        both_halves(f, claim(f)[:, 0:2 * P], b, lambda c: cT[:, :, c, t])
                    elif stage == CONTEXT:
                        pe.wait_ge(drained, grp(SIM, b) + 1)
                        split_mm(claim(f), p_hi[:, b, :], p_lo[:, b, :], c_hi[:, b, :], c_lo[:, b, :],
                                 True, True).then_inc(filled, 1)
                    elif stage == LN2_T:
                        pe.wait_ge(xn_ready, B + b + 1)
                        transpose_tile(f, b)
                    elif stage == EXPERTS:
                        product(f, claim(f), b, xT_hi, xT_lo, lambda c: a_hi[:, c, :], lambda c: a_lo[:, c, :])
                    elif stage == GATED_T:
                        pe.wait_ge(drained, grp(EXPERTS, b) + 1)
                        transpose_tile(f, b)
                    elif stage == MIX:
                        pe.wait_ge(drained, grp(GATED_T, b) + 1)
                        product(f, claim(f), b, zT_hi, zT_lo, lambda c: b_hi[:, c, :], lambda c: b_lo[:, c, :])
                    elif h == 0:
                        pe.wait_ge(y_ready, b + 1)
                        transpose_tile(f, b, y0)
            pe.wait_ge(drained, grp(MIX, B - 1) + 1)

            pe.sem_inc(fill_free, 3)

            def transpose_p(i, u):
                pe.wait_ge(p_s, i * 4 + u)
                for b in range(HB):
                    last = pe.transpose(PS[2][:, b * P:(b + 1) * P], E[:, b, :], ident[:])
                last.then_inc(pt_done, 1)

            def attend(i, u, first=False):
                h, t = unit((u - 1) % 4)
                v = slice(h * DH, (h + 1) * DH)
                pe.wait_ge(pt_lo_s, i * 4 + u)
                if h == 0:
                    pe.wait_ge(fill_free, 3 + fills(i, V_FILLS[2 * t][1], first))
                for b in range(HB):
                    n = HB * t + b
                    pe.matmul(sc[:, b, :], v_hi[:, n, v], pp[:, b, :], start=True, stop=False)
                    last = pe.matmul(sc[:, b, :], v_lo[:, n, v], pp[:, b, :], start=False, stop=True)
                last.then_inc(pv_done, 1)

            def output_tile(i, k, h, first=False):
                n = k + 2 if k < 6 else k - 8
                if h == 0 and fill_bank(i, k, first) > 0:
                    pe.wait_ge(fill_free, fills(i, k, first))
                t = slice(n * P, (n + 1) * P)
                w = slice(h * D, (h + 1) * D)
                last = split_mm(PS[fill_bank(i, k, first)], at_hi[:, h, t], at_lo[:, h, t], w_hi[WO][:, w],
                                w_lo[WO][:, w], h == 0, h == 1)
                if h == 1:
                    last.then_inc(fill_done, 1)

            def pair(i, first=False):
                def project(u, s):
                    h, half_ = unit(u)
                    hi, lo = (xT_hi, xT_lo) if s == 0 else (cT_hi, cT_lo)
                    t = slice(HALF * half_, HALF * half_ + HALF)
                    for c in range(DC):
                        w = slice((s * DC + c) * P, (s * DC + c + 1) * P)
                        last = split_mm(PS[s], w_hi[h][:, w], w_lo[h][:, w], hi[:, c, t], lo[:, c, t],
                                        c == 0, c == DC - 1)
                    last.then_inc(qk_done, 1)

                def value(k, part):
                    a, cs = part // 2, range(DC // 2 * (part % 2), DC // 2 * (part % 2 + 1))
                    n = 2 * (k if k < 2 else k - 4) + a
                    if part == 0:
                        pe.wait_ge(fill_free, fills(i, k, first))
                    t = slice(n * P, (n + 1) * P)
                    for c in cs:
                        w = slice(c * 256, (c + 1) * 256)
                        last = split_mm(PS[fill_bank(i, k, first)][:, a * 256:(a + 1) * 256], cT_hi[:, c, t],
                                        cT_lo[:, c, t], w_hi[WV][:, w], w_lo[WV][:, w], c == 0, c == DC - 1)
                    if part == 3:
                        last.then_inc(fill_done, 1)

                def scores(u):
                    pe.wait_ge(qk_lo_s, i * 8 + (2 * u + 2))
                    if u > 0 or not first:
                        pe.wait_ge(pv_summed, i * 4 + u)
                    for b in range(HB):
                        t = slice(b * P, (b + 1) * P)
                        pe.matmul(sc[:, b, :], q_hi[:, t], kk[:, b, :], start=True, stop=False)
                        last = pe.matmul(sc[:, b, :], q_lo[:, t], kk[:, b, :], start=False, stop=True)
                    last.then_inc(sc_done, 1)

                def input_tile(b):
                    pe.wait_ge(y_ready, b + 1)
                    transpose_tile(grp(LN3_T, b), b)

                def row_fills(u, eighth):
                    if u in V_FILLS:
                        value(V_FILLS[u][eighth // 4], eighth % 4)
                    elif u == 3 or not first:
                        output_tile(i, O_FILLS[u][eighth // 2], eighth % 2, first)

                if first:
                    pe.wait_ge(w_ready[WV], i + 1)
                    for eighth in range(4):
                        row_fills(0, eighth)
                    pe.wait_ge(drained, grp(LN3_T, HB - 1) + 1)
                for u in range(4):
                    if first and u == 2:
                        pe.wait_ge(drained, LAST0 + 1)
                    if u < 2:
                        pe.wait_ge(w_ready[u], i + 1)
                    project(u, 0)
                    if u > 0 or not first:
                        transpose_p(i, u)
                    project(u, 1)
                    if first and u == 1:
                        pe.wait_ge(fill_free, 3 + fills(i, V_FILLS[0][1], first))
                        input_tile(4)
                        input_tile(5)
                    if u > 0 or not first:
                        attend(i, u, first)
                    if first and u == 1:
                        input_tile(6)
                        input_tile(7)
                    if u == 0:
                        pe.wait_ge(w_ready[WV], i + 1)
                    if u == 1 and not first:
                        pe.wait_ge(at_lo_s, i * 4)
                    if u == 3:
                        pe.wait_ge(w_ready[WO], i + 1)
                        pe.wait_ge(at_lo_s, i * 4 + 2)
                    start, cut_at = (4, 6) if first and u == 0 else (0, 3)
                    for eighth in range(start, cut_at):
                        row_fills(u, eighth)
                    scores(u)
                    for eighth in range(cut_at, 8):
                        row_fills(u, eighth)

            pair(0, first=True)
            with pe.Fori(1, PAIRS) as i:
                pair(i)
            output_tile(PAIRS, 2, 0)
            output_tile(PAIRS, 3, 0)
            transpose_p(PAIRS, 0)
            output_tile(PAIRS, 4, 0)
            output_tile(PAIRS, 5, 0)
            attend(PAIRS, 0)
            pe.wait_ge(at_lo_s, 4 * PAIRS)
            output_tile(PAIRS, 2, 1)
            output_tile(PAIRS, 3, 1)
            for b in half(0):
                pe.wait_ge(xn_ready, 3 * B + b + 1)
                transpose_tile(LN4 + b, b)
            output_tile(PAIRS, 4, 1)
            output_tile(PAIRS, 5, 1)
            pe.wait_ge(drained, LN4 + HB)

            def hidden(j, t):
                at = slice(HALF * t, HALF * t + HALF)
                for m in range(2):
                    for c in range(DC):
                        w = slice((m * DC + c) * P, (m * DC + c + 1) * P)
                        last = split_mm(PS[hid_bank(t, m)], f_hi[:, w], f_lo[:, w], xT_hi[:, c, at],
                                        xT_lo[:, c, at], c == 0, c == DC - 1)
                    last.then_inc(ab_done, 1)

            def out(j):
                pe.wait_ge(f2_ready, j + 1)
                for n in range(B):
                    if n in (0, 4, 6):
                        pe.wait_ge(h_lo_s, j * 3 + (0, 4, 6).index(n) + 1)
                    pe.wait_ge(o_free, j * 8 + (n + 1))
                    t = slice(n * P, (n + 1) * P)
                    w = slice(2 * DC * P, CHUNK)
                    split_mm(PS[4 + n % 4], h_hi[:, t], h_lo[:, t], f_hi[:, w], f_lo[:, w], True, True
                             ).then_inc(o_done, 1)

            pe.wait_ge(f13_ready, 1)
            hidden(0, 0)
            pe.wait_ge(fill_free, 3 + 12 * PAIRS)
            for b in half(1):
                pe.wait_ge(xn_ready, 3 * B + b + 1)
                transpose_tile(LN4 + b, b)
            pe.wait_ge(drained, LN4 + B)
            pe.sem_inc(o_free, 4)
            hidden(0, 1)
            out(0)
            with pe.Fori(1, HC) as j:
                pe.wait_ge(f13_ready, j + 1)
                hidden(j, 0)
                hidden(j, 1)
                out(j)


def _layouts(np, a):
    f = np.ascontiguousarray
    ctx = a["ctx_4096"]
    small = np.empty((P, 4), np.float32)
    small[:, 0:2] = a["g_xattn"]
    small[:, 2:4] = a["g_ffn"]
    by_width = lambda w: w.T.reshape(DC, P, -1).transpose(1, 0, 2)
    ab = np.concatenate([by_width(a["L0_ffn_A_w"]).reshape(P, -1), by_width(a["L0_ffn_B_w"]).reshape(P, -1)], 1)
    q, k, v = (by_width(a[f"L1_xattn_w_{n}"]).reshape(P, DC, PAIRS, 2, DH) for n in "qkv")
    weights = np.empty((PAIRS, P, 4, BLK), np.float32)
    for h in range(2):
        qk = np.stack([q[:, :, :, h], k[:, :, :, h]])
        weights[:, :, QK0 + h] = qk.transpose(3, 1, 0, 2, 4).reshape(PAIRS, P, BLK)
    weights[:, :, WV] = v.transpose(2, 0, 1, 3, 4).reshape(PAIRS, P, BLK)
    o = a["L1_xattn_w_out"].T.reshape(PAIRS, 2, DH, D)
    weights[:, :, WO] = o.transpose(0, 2, 1, 3).reshape(PAIRS, P, BLK)
    bias = a["L1_xattn_position_bias"].reshape(PAIRS, 2, P, P).transpose(0, 2, 1, 3)

    def spread(packed, s, rows, cols):
        n = np.arange(rows * cols).reshape(rows, cols)
        return packed[n // 128, n % 64].T, s[n // 64].T

    words = np.zeros((HC, P, CHUNK + SHIFTS), np.int32)
    scales = np.zeros((HC, P, CHUNK), np.float32)

    def hidden_chunks(m):
        m = np.pad(m, ((0, 0), (0, HC * P - HID)))
        return m.reshape(DC, P, HC, P).transpose(2, 1, 0, 3).reshape(HC, P, DC * P)

    for at, n in ((0, "1"), (DC * P, "3")):
        w, s = spread(a[f"L1_ffn_w{n}"], a[f"L1_ffn_s{n}"], HID, D)
        words[:, :, at:at + DC * P] = hidden_chunks(w)
        scales[:, :, at:at + DC * P] = hidden_chunks(s)
    w, s = spread(a["L1_ffn_w2"], a["L1_ffn_s2"], D, HID)
    words[:, :, 2 * DC * P:CHUNK] = np.pad(w, ((0, HC * P - HID), (0, 0))).reshape(HC, P, D)
    scales[:, :, 2 * DC * P:] = np.pad(s, ((0, HC * P - HID), (0, 0))).reshape(HC, P, D)
    low13 = (np.arange(P) // 64 % 2)[None, :, None]
    hid = np.arange(HC * P).reshape(HC, P)
    low2 = (hid[:, :, None] + HID * np.arange(4)) // 64 % 2
    low = np.concatenate([np.broadcast_to(low13, (HC, P, 1)), low2], 2)
    words[:, :, CHUNK:] = np.stack([28 * low, 4 + 24 * low], 3).reshape(HC, P, SHIFTS)
    return {
        "x": f(a["x"]), "ctx": f(ctx), "ctxT": f(ctx.reshape(T, D).T),
        "mask": f(a["mask_BxSxS2_bk0"]), "small": small,
        "norm_w": f(np.broadcast_to(a["L1_xattn_ln_weight"], (P, D))),
        "wq_r": f(a["L0_ffn_Wq_w"]), "keysT": f(a["L0_ffn_keys"].T), "ab": f(ab),
        "weights": f(weights.reshape(PAIRS, P, 4 * BLK)), "bias": f(bias),
        "words": words, "scales": scales,
    }


def kernel(**inputs):
    import numpy as np
    from concourse import bacc
    from concourse.bass_utils import run_bass_kernel_spmd

    arrays = _layouts(np, {k: np.asarray(v) for k, v in inputs.items()})
    nc = bacc.Bacc("TRN2", target_bir_lowering=False, num_devices=1)
    aps = {k: nc.dram_tensor(f"in_{k}", v.shape, mybir.dt.from_np(v.dtype), kind="ExternalInput").ap()
           for k, v in arrays.items()}
    out = nc.dram_tensor("out_x", (B, P, D), F32, kind="ExternalOutput").ap()
    gated_layers(nc, out=out, **aps)
    result = run_bass_kernel_spmd(nc, [{f"in_{k}": v for k, v in arrays.items()}], core_ids=[0])
    return result.results[0]["out_x"]
```
